# Optimizing a Trainium2 kernel written in Bass

```python
import numpy as np
import jax
import jax.numpy as jnp

def _softmax(x, axis=-1):
    return jax.nn.softmax(x, axis=axis)

def _gelu(x):
    return jax.nn.gelu(x, approximate=True)

def _silu(x):
    return jax.nn.silu(x)

def _sigmoid(x):
    return jax.nn.sigmoid(x)

def _layernorm(x, axis=-1, eps=1e-05):
    m = jnp.mean(x, axis=axis, keepdims=True)
    v = jnp.var(x, axis=axis, keepdims=True)
    return (x - m) / jnp.sqrt(v + eps)

def _scatter_add(tgt, idx, src, axis=0):
    return tgt.at[idx].add(src)

def _segment_sum(src, seg, n):
    return jax.ops.segment_sum(src, seg, n)
kernel_name = 'mk_hybrid_d1_jaxref_r8_546ebc'

def setup_inputs(seed: int=0):
    np.random.seed(seed)
    _w = jnp.asarray

    def _L0_attn_a_setup():
        import jax, jax.numpy as jnp
        import numpy as np
        import math
        H = 16
        EPS = 1e-05
        key = jax.random.key(seed)
        ks = jax.random.split(key, 4)
        B, T, D = (2, 256, 128)
        s = 1.0 / math.sqrt(D)
        return {'x': jax.random.normal(ks[0], (B, T, D), dtype=jnp.float32), 'ln_g': jnp.ones((D,), jnp.float32), 'ln_b': jnp.zeros((D,), jnp.float32), 'Wq': jax.random.normal(ks[1], (D, D), jnp.float32) * s, 'bq': jnp.zeros((D,), jnp.float32), 'Wk': jax.random.normal(ks[2], (D, D), jnp.float32) * s, 'bk': jnp.zeros((D,), jnp.float32), 'Wv': jax.random.normal(ks[3], (D, D), jnp.float32) * s, 'bv': jnp.zeros((D,), jnp.float32)}
    _L0_attn_a_in = _L0_attn_a_setup()

    def _L0_attn_b_setup():
        import jax, jax.numpy as jnp
        import numpy as np
        B, S, E, H = (2, 256, 128, 16)
        key = jax.random.key(seed)
        k1, k2 = jax.random.split(key)
        inputs = jax.random.normal(k1, (B, S, E), dtype=jnp.float32)
        qkv_kernel = jax.random.normal(k2, (E, 3 * E), dtype=jnp.float32) * (1.0 / np.sqrt(E))
        qkv_bias = jnp.zeros((1, 3 * E), dtype=jnp.float32)
        return {'inputs': inputs, 'qkv_kernel': qkv_kernel, 'qkv_bias': qkv_bias}
    _L0_attn_b_in = _L0_attn_b_setup()

    def _L0_ffn_setup():
        import jax, jax.numpy as jnp
        import numpy as np
        D_MODEL = 128
        D1, D2 = (32, 32)
        F1, F2 = (64, 64)
        E = 64
        TOP_K = 2

        def kmoe(x_flat, W_router, A, B, scale, bias, d_in1, d_in2, d_out1, d_out2, top_k):
            logits = x_flat @ W_router.T
            vals, idx = jax.lax.top_k(logits, top_k)
            probs = jax.nn.softmax(vals, axis=-1)
            xs = x_flat.reshape(-1, d_in1, d_in2)
            Ag = A[idx]
            Bg = B[idx]
            Y = jnp.einsum('nkoi,nij,nkpj->nkop', Ag, xs, Bg)
            out = jnp.einsum('nkop,nk->nop', Y, probs).reshape(-1, d_out1 * d_out2)
            return out * scale + bias
        key = jax.random.key(seed)
        ks = jax.random.split(key, 12)
        s = 0.02
        return {'x': jax.random.normal(ks[0], (4, 256, D_MODEL), dtype=jnp.float32), 'W_up': jax.random.normal(ks[1], (E, D1 * D2), dtype=jnp.float32) * s, 'A_up': jax.random.normal(ks[2], (E, F1, D1), dtype=jnp.float32) * s, 'B_up': jax.random.normal(ks[3], (E, F2, D2), dtype=jnp.float32) * s, 'scale_up': jnp.ones((1,), dtype=jnp.float32), 'bias_up': jnp.zeros((F1 * F2,), dtype=jnp.float32), 'W_down': jax.random.normal(ks[4], (E, F1 * F2), dtype=jnp.float32) * s, 'A_down': jax.random.normal(ks[5], (E, D1, F1), dtype=jnp.float32) * s, 'B_down': jax.random.normal(ks[6], (E, D2, F2), dtype=jnp.float32) * s, 'scale_down': jnp.ones((1,), dtype=jnp.float32), 'bias_down': jnp.zeros((D1 * D2,), dtype=jnp.float32)}
    _L0_ffn_in = _L0_ffn_setup()
    _d = {'L0_attn_a_x': _L0_attn_a_in['x'], 'L0_attn_a_ln_g': _L0_attn_a_in['ln_g'], 'L0_attn_a_ln_b': _L0_attn_a_in['ln_b'], 'L0_attn_a_Wq': _L0_attn_a_in['Wq'], 'L0_attn_a_bq': _L0_attn_a_in['bq'], 'L0_attn_a_Wk': _L0_attn_a_in['Wk'], 'L0_attn_a_bk': _L0_attn_a_in['bk'], 'L0_attn_a_Wv': _L0_attn_a_in['Wv'], 'L0_attn_a_bv': _L0_attn_a_in['bv'], 'L0_attn_b_qkv_kernel': _L0_attn_b_in['qkv_kernel'], 'L0_attn_b_qkv_bias': _L0_attn_b_in['qkv_bias'], 'L0_ffn_W_up': _L0_ffn_in['W_up'], 'L0_ffn_A_up': _L0_ffn_in['A_up'], 'L0_ffn_B_up': _L0_ffn_in['B_up'], 'L0_ffn_scale_up': _L0_ffn_in['scale_up'], 'L0_ffn_bias_up': _L0_ffn_in['bias_up'], 'L0_ffn_W_down': _L0_ffn_in['W_down'], 'L0_ffn_A_down': _L0_ffn_in['A_down'], 'L0_ffn_B_down': _L0_ffn_in['B_down'], 'L0_ffn_scale_down': _L0_ffn_in['scale_down'], 'L0_ffn_bias_down': _L0_ffn_in['bias_down']}
    _x0 = _d['L0_attn_a_x']
    _d['L0_attn_a_x'] = jax.random.normal(jax.random.fold_in(jax.random.key(seed), 1), (2, 1024, 128), dtype=_x0.dtype)
    del _x0
    return _d

def reference(L0_attn_a_x, L0_attn_a_ln_g, L0_attn_a_ln_b, L0_attn_a_Wq, L0_attn_a_bq, L0_attn_a_Wk, L0_attn_a_bk, L0_attn_a_Wv, L0_attn_a_bv, L0_attn_b_qkv_kernel, L0_attn_b_qkv_bias, L0_ffn_W_up, L0_ffn_A_up, L0_ffn_B_up, L0_ffn_scale_up, L0_ffn_bias_up, L0_ffn_W_down, L0_ffn_A_down, L0_ffn_B_down, L0_ffn_scale_down, L0_ffn_bias_down):

    def _L0_attn_a_ref(x, ln_g, ln_b, Wq, bq, Wk, bk, Wv, bv):
        import jax, jax.numpy as jnp
        import numpy as np
        import math
        H = 16
        EPS = 1e-05
        B, T, D = x.shape
        mu = jnp.mean(x, axis=-1, keepdims=True)
        var = jnp.mean(jnp.square(x - mu), axis=-1, keepdims=True)
        xn = (x - mu) * jax.lax.rsqrt(var + EPS) * ln_g + ln_b
        q = (xn @ Wq + bq).reshape(B, T, H, D // H)
        k = (xn @ Wk + bk).reshape(B, T, H, D // H)
        v = (xn @ Wv + bv).reshape(B, T, H, D // H)
        scale = 1.0 / math.sqrt(D // H)
        attn = jnp.einsum('bnhd,bmhd->bnmh', q, k) * scale
        w = jax.nn.softmax(attn, axis=2)
        y = jnp.einsum('bnmh,bmhd->bnhd', w, v).reshape(B, T, D)
        return y

    def _L0_attn_b_ref(inputs, qkv_kernel, qkv_bias):
        import jax, jax.numpy as jnp
        import numpy as np
        B, S, E, H = (2, 256, 128, 16)
        b, s, e = inputs.shape
        hidden, heads = (E, H)
        qkv = jnp.einsum('bse,ef->bsf', inputs, qkv_kernel) + qkv_bias
        qkv_heads = qkv.reshape(b, heads, s, -1)
        q, k, v = jnp.split(qkv_heads, 3, axis=-1)
        scale = 1.0 / np.sqrt(2.0 * hidden)
        qk = jnp.einsum('bhse,bhte->bhst', q, k) * scale
        mask = jnp.triu(jnp.full((s, s), -jnp.inf, dtype=jnp.float32), k=1)
        attn = jax.nn.softmax(qk + mask, axis=-1)
        out = jnp.einsum('bhst,bhte->bhse', attn, v).reshape(b, s, e)
        return out

    def _L0_ffn_ref(x, W_up, A_up, B_up, scale_up, bias_up, W_down, A_down, B_down, scale_down, bias_down):
        import jax, jax.numpy as jnp
        import numpy as np
        D_MODEL = 128
        D1, D2 = (32, 32)
        F1, F2 = (64, 64)
        E = 64
        TOP_K = 2

        def kmoe(x_flat, W_router, A, B, scale, bias, d_in1, d_in2, d_out1, d_out2, top_k):
            logits = x_flat @ W_router.T
            vals, idx = jax.lax.top_k(logits, top_k)
            probs = jax.nn.softmax(vals, axis=-1)
            xs = x_flat.reshape(-1, d_in1, d_in2)
            Ag = A[idx]
            Bg = B[idx]
            Y = jnp.einsum('nkoi,nij,nkpj->nkop', Ag, xs, Bg)
            out = jnp.einsum('nkop,nk->nop', Y, probs).reshape(-1, d_out1 * d_out2)
            return out * scale + bias
        orig_shape = x.shape
        x_flat = x.reshape(-1, D1 * D2)
        h = kmoe(x_flat, W_up, A_up, B_up, scale_up, bias_up, D1, D2, F1, F2, TOP_K)
        h = jax.nn.gelu(h, approximate=False)
        y = kmoe(h, W_down, A_down, B_down, scale_down, bias_down, F1, F2, D1, D2, TOP_K)
        return y.reshape(*orig_shape[:-1], D_MODEL)
    x = L0_attn_a_x
    x = x + _L0_attn_a_ref(_layernorm(x, axis=-1), L0_attn_a_ln_g, L0_attn_a_ln_b, L0_attn_a_Wq, L0_attn_a_bq, L0_attn_a_Wk, L0_attn_a_bk, L0_attn_a_Wv, L0_attn_a_bv)
    x = x + _L0_ffn_ref(_layernorm(x, axis=-1), L0_ffn_W_up, L0_ffn_A_up, L0_ffn_B_up, L0_ffn_scale_up, L0_ffn_bias_up, L0_ffn_W_down, L0_ffn_A_down, L0_ffn_B_down, L0_ffn_scale_down, L0_ffn_bias_down)
    x = x + _L0_attn_b_ref(_layernorm(x, axis=-1), L0_attn_b_qkv_kernel, L0_attn_b_qkv_bias)
    x = x + _L0_ffn_ref(_layernorm(x, axis=-1), L0_ffn_W_up, L0_ffn_A_up, L0_ffn_B_up, L0_ffn_scale_up, L0_ffn_bias_up, L0_ffn_W_down, L0_ffn_A_down, L0_ffn_B_down, L0_ffn_scale_down, L0_ffn_bias_down)
    return x

_drawn_inputs = setup_inputs


def setup_inputs(seed=0):
    import zlib

    import numpy as np

    out = dict(_drawn_inputs(seed))
    spreads = {'L0_attn_a_ln_g': (1.0, 0.2),
     'L0_attn_a_ln_b': (0.0, 0.1),
     'L0_attn_a_bq': (0.0, 0.699),
     'L0_attn_a_bk': (0.0, 0.8),
     'L0_attn_a_bv': (0.0, 0.1),
     'L0_attn_b_qkv_bias': (0.0, 0.1),
     'L0_ffn_bias_up': (0.0, 0.8),
     'L0_ffn_bias_down': (0.0, 0.1)}
    factors = {'L0_ffn_W_up': 8.0,
     'L0_ffn_A_up': 8.0,
     'L0_ffn_B_up': 8.0,
     'L0_ffn_W_down': 8.0,
     'L0_ffn_A_down': 8.0,
     'L0_ffn_B_down': 8.0}
    for name, (base, spread) in spreads.items():
        noise = np.random.default_rng([zlib.crc32(name.encode()), seed]).standard_normal(out[name].shape)
        drawn = base * np.exp(spread * noise) if base else spread * noise
        out[name] = jnp.asarray(drawn.astype(out[name].dtype))
    for name, factor in factors.items():
        out[name] = (out[name] * factor).astype(out[name].dtype)
    return out
```

```python
from contextlib import ExitStack

import concourse.bass as bass
from concourse import mybir

F32 = mybir.dt.float32
BF16 = mybir.dt.bfloat16
U32 = mybir.dt.uint32
ALU = mybir.AluOpType
ACT = mybir.ActivationFunctionType
AXX = mybir.AxisListType.X

P = 128
BATCH, SEQ, D = 2, 1024, 128
HEADS, HD = 16, 8
TILES = BATCH * SEQ // P
TPB = SEQ // P
QUADS = BATCH * HEADS // 4
EXPERTS = 64
D1, F1 = 32, 64
TOKROWS = D1 * D1 // D
EPS = 1e-5
MASKED = -1e30
BANK = 512
STACK = 64
STACK_USED = 56


class Kernel:
    def __init__(self, nc, a, out):
        self.nc, self.a, self.out = nc, a, out
        self.names = 0

    def sem(self, ctx, name):
        self.names += 1
        return ctx.enter_context(self.nc.semaphore(f"{name}_{self.names}"))

    def sb(self, ctx, name, shape, dt=F32):
        self.names += 1
        return ctx.enter_context(self.nc.sbuf_tensor(f"{name}_{self.names}", shape, dt))

    def banks(self, ctx, n=8):
        self.names += 1
        return [ctx.enter_context(self.nc.psum_tensor(f"bank{i}_{self.names}", [P, BANK], F32)) for i in range(n)]

    def setup(self, ctx):
        nc, a = self.nc, self.a
        sb = self.sb
        self.x = sb(ctx, "x", [P, TILES, D])
        self.ident = sb(ctx, "ident", [P, P])
        self.identb = sb(ctx, "identb", [P, P], BF16)
        self.mask_qk = sb(ctx, "mask_qk", [P, P], BF16)
        self.mask_kq = sb(ctx, "mask_kq", [P, P], BF16)
        self.half_neg = sb(ctx, "half_neg", [P, TILES])
        self.iota_e = sb(ctx, "iota_e", [P, EXPERTS])
        self.w_qkv = sb(ctx, "w_qkv", [P, 3 * D])
        self.w_qkv_b = sb(ctx, "w_qkv_b", [P, 3 * D])
        self.b_qkv = sb(ctx, "b_qkv", [P, 3 * D])
        self.b_qkv_b = sb(ctx, "b_qkv_b", [P, 3 * D])
        self.ln_g = sb(ctx, "ln_g", [P, 1])
        self.ln_b = sb(ctx, "ln_b", [P, 1])
        self.router_up = sb(ctx, "router_up", [P, TOKROWS, EXPERTS])
        self.router_dn = sb(ctx, "router_dn", [P, F1, EXPERTS])
        self.tab = {k: sb(ctx, k, [EXPERTS, F1 * D1]) for k in ("A_up", "B_up", "A_down", "B_down")}
        self.bias_up = sb(ctx, "bias_up", [P, F1])
        self.bias_dn = sb(ctx, "bias_dn", [P, D1])
        self.scale_up = sb(ctx, "scale_up", [P, 1])
        self.scale_dn = sb(ctx, "scale_dn", [P, 1])

        with ExitStack() as c:
            wu = sb(c, "wu", [EXPERTS, D1 * D1])
            wd = sb(c, "wd", [EXPERTS, F1 * F1])
            bu = sb(c, "bu", [F1, F1])
            bd = sb(c, "bd", [D1, D1])
            bank = self.banks(c)
            x_in, loaded, chain, const = (self.sem(c, n) for n in ("x_in", "loaded", "chain", "const"))
            filled, evacuated = self.sem(c, "filled"), self.sem(c, "evacuated")
            block = c.enter_context(nc.Block())
            JOBS = 1 + F1 // 8 + 1

            @block.sync
            def _(sp):
                sp.dma_start(self.x[:], a["L0_attn_a_x"].rearrange("b (t p) d -> p (b t) d", p=P)).then_inc(x_in, 16)
                sp.dma_start(wu[:], a["L0_ffn_W_up"]).then_inc(loaded, 16)
                sp.dma_start(wd[:], a["L0_ffn_W_down"]).then_inc(loaded, 16)
                sp.dma_start(bu[:], a["L0_ffn_bias_up"].rearrange("(o p) -> o p", p=F1)).then_inc(loaded, 16)
                sp.dma_start(bd[:], a["L0_ffn_bias_down"].rearrange("(o p) -> o p", p=D1)).then_inc(loaded, 16)
                for n, k in enumerate(("Wq", "Wk", "Wv")):
                    sp.dma_start(self.w_qkv[:, n * D:(n + 1) * D], a["L0_attn_a_" + k]).then_inc(x_in, 16)
                sp.dma_start(self.w_qkv_b[:], a["L0_attn_b_qkv_kernel"]).then_inc(x_in, 16)
                for k in ("A_up", "B_up", "A_down", "B_down"):
                    sp.dma_start(self.tab[k][:], a["L0_ffn_" + k].rearrange("e o i -> e (o i)")).then_inc(x_in, 16)
                sp.wait_ge(x_in, 9 * 16)

            @block.scalar
            def _(act):
                for n, k in enumerate(("bq", "bk", "bv")):
                    act.dma_start(self.b_qkv[:, n * D:(n + 1) * D],
                                  a["L0_attn_a_" + k].partition_broadcast(P)).then_inc(const, 16)
                act.dma_start(self.b_qkv_b[:], a["L0_attn_b_qkv_bias"][0].partition_broadcast(P)).then_inc(const, 16)
                act.dma_start(self.ln_g[:], a["L0_attn_a_ln_g"].rearrange("(p o) -> p o", o=1)).then_inc(const, 16)
                act.dma_start(self.ln_b[:], a["L0_attn_a_ln_b"].rearrange("(p o) -> p o", o=1)).then_inc(const, 16)
                act.dma_start(self.scale_up[:], a["L0_ffn_scale_up"].partition_broadcast(P)).then_inc(const, 16)
                act.dma_start(self.scale_dn[:], a["L0_ffn_scale_down"].partition_broadcast(P)).then_inc(const, 16)
                act.wait_ge(const, 8 * 16)

            @block.gpsimd
            def _(pool):
                nc.gpsimd.memset(self.ident[:], 0.0).then_inc(chain, 1)
                nc.gpsimd.memset(self.identb[:], 0.0).then_inc(chain, 1)
                nc.gpsimd.memset(self.mask_qk[:], 0.0).then_inc(chain, 1)
                nc.gpsimd.memset(self.mask_kq[:], 0.0).then_inc(chain, 1)
                nc.gpsimd.memset(self.half_neg[:], -0.5).then_inc(chain, 1)
                nc.gpsimd.iota(self.iota_e[:], pattern=[[1, EXPERTS]], base=0, channel_multiplier=0,
                               allow_small_or_imprecise_dtypes=True).then_inc(chain, 1)
                pool.wait_ge(chain, 6)
                for m in (self.ident, self.identb):
                    nc.gpsimd.affine_select(out=m[:], in_=m[:], pattern=[[-1, P]], compare_op=ALU.not_equal,
                                            fill=1.0, base=0, channel_multiplier=1).then_inc(chain, 1)
                nc.gpsimd.affine_select(out=self.mask_qk[:], in_=self.mask_qk[:], pattern=[[-1, P]],
                                        compare_op=ALU.is_ge, fill=MASKED, base=0,
                                        channel_multiplier=1).then_inc(chain, 1)
                nc.gpsimd.affine_select(out=self.mask_kq[:], in_=self.mask_kq[:], pattern=[[1, P]],
                                        compare_op=ALU.is_ge, fill=MASKED, base=0,
                                        channel_multiplier=-1).then_inc(chain, 1)

            @block.tensor
            def _(pe):
                pe.wait_ge(chain, 10)
                pe.wait_ge(loaded, 4 * 16)
                for r in range(TOKROWS):
                    last = nc.tensor.transpose(bank[0][:, r * 64:(r + 1) * 64], wu[:, r * D:(r + 1) * D],
                                               self.ident[0:64, 0:64])
                last.then_inc(filled, 1)
                for j in range(F1 // 8):
                    if j == 7:
                        pe.wait_ge(evacuated, 1)
                    for o in range(8):
                        for half in range(2):
                            last = nc.tensor.matmul(bank[(1 + j) % 8][64 * half:64 * half + 64, o * 64:(o + 1) * 64],
                                                    wd[:, (8 * j + o) * 64:(8 * j + o + 1) * 64],
                                                    self.ident[0:64, 0:64], start=True, stop=True)
                    last.then_inc(filled, 1)
                pe.wait_ge(evacuated, 2)
                for half in range(2):
                    nc.tensor.matmul(bank[1][64 * half:64 * half + 64, 0:F1], bu[:], self.ident[0:64, 0:64],
                                     start=True, stop=True)
                for g in range(4):
                    last = nc.tensor.matmul(bank[1][32 * g:32 * g + 32, F1:F1 + D1], bd[:], self.ident[0:32, 0:32],
                                            start=True, stop=True)
                last.then_inc(filled, 1)

            @block.vector
            def _(dve):
                for j in range(JOBS):
                    dve.wait_ge(filled, j + 1)
                    b = bank[j % 8]
                    if j == 0:
                        nc.vector.tensor_copy(self.router_up[:].rearrange("p r e -> p (r e)"), b[:]).then_inc(evacuated, 1)
                    elif j < JOBS - 1:
                        nc.vector.tensor_copy(self.router_dn[:, 8 * (j - 1):8 * j, :].rearrange("p o e -> p (o e)"),
                                              b[:]).then_inc(evacuated, 1)
                    else:
                        nc.vector.tensor_copy(self.bias_up[:], b[:, 0:F1]).then_inc(evacuated, 1)
                        nc.vector.tensor_copy(self.bias_dn[:], b[:, F1:F1 + D1]).then_inc(evacuated, 1)

    def layernorm_dve(self, dve, src, dst, s, tag):
        nc = self.nc
        for t in range(TILES):
            nc.vector.bn_stats(s["stats"][:, t, :], src[:, t, :]).then_inc(s["stat_done"], 1)
        dve.wait_ge(s["stat_done"], (2 * tag + 1) * TILES)
        for t in range(TILES):
            nc.vector.bn_aggr(s["meanvar"][:, t, :], s["stats"][:, t, :]).then_inc(s["stat_done"], 1)
        dve.wait_ge(s["rstd_done"], 2 * tag + 2)
        for t in range(TILES):
            nc.vector.tensor_scalar(dst[:, t, :], src[:, t, :], s["meanvar"][:, t, 0:1], s["rstd"][:, t:t + 1],
                                    ALU.subtract, ALU.mult).then_inc(s["normed"], 1)

    def layernorm_pool(self, pool, s, tag):
        nc = self.nc
        pool.wait_ge(s["stat_done"], (2 * tag + 2) * TILES)
        nc.gpsimd.tensor_scalar(s["rstd"][:], s["meanvar"][:, :, 1], EPS, None, ALU.add).then_inc(s["rstd_done"], 1)
        pool.wait_ge(s["rstd_done"], 2 * tag + 1)
        nc.gpsimd.tensor_tensor(s["rstd"][:], s["rstd"][:], self.half_neg[:], ALU.pow).then_inc(s["rstd_done"], 1)

    def layernorm_state(self, c):
        s = {n: self.sem(c, n) for n in ("stat_done", "rstd_done", "normed")}
        s["stats"] = self.sb(c, "stats", [P, TILES, 6])
        s["meanvar"] = self.sb(c, "meanvar", [P, TILES, 2])
        s["rstd"] = self.sb(c, "rstd", [P, TILES])
        return s

    def project(self, causal, qkv):
        nc = self.nc
        with ExitStack() as c:
            xn = self.sb(c, "xn", [P, TILES, D])
            xt = self.sb(c, "xt", [P, TILES, P])
            rows = self.sb(c, "rows", [P, TILES, 3 * D]) if causal else None
            s = self.layernorm_state(c)
            bank = self.banks(c)
            filled, by_dve, by_act = (self.sem(c, n) for n in ("filled", "by_dve", "by_act"))
            stored, back = self.sem(c, "stored"), self.sem(c, "back")
            block = c.enter_context(nc.Block())
            w = self.w_qkv_b if causal else self.w_qkv
            bias = self.b_qkv_b if causal else self.b_qkv
            norms = 1 if causal else 2
            TJ = TILES // 4

            @block.tensor
            def _(pe):
                for j in range(TJ):
                    for t in range(4 * j, 4 * j + 4):
                        pe.wait_ge(s["normed"], (norms - 1) * TILES + t + 1)
                        last = nc.tensor.transpose(bank[j][:, (t % 4) * P:(t % 4 + 1) * P], xn[:, t, :], self.ident[:])
                    last.then_inc(filled, 1)
                for t in range(TILES):
                    if t % 4 == 0:
                        pe.wait_ge(by_act, t // 4 + 1)
                    if t >= 4:
                        pe.wait_ge(by_dve, t - 3)
                    nc.tensor.matmul(bank[4 + t % 4][:, 0:3 * D], xt[:, t, :], w[:], start=True,
                                     stop=True).then_inc(filled, 1)

            @block.scalar
            def _(act):
                for j in range(TJ):
                    act.wait_ge(filled, j + 1)
                    dst = xt[:, 4 * j:4 * j + 4, :].rearrange("p t r -> p (t r)")
                    if causal:
                        nc.scalar.activation(dst, bank[j][:], ACT.Identity).then_inc(by_act, 1)
                    else:
                        nc.scalar.activation(dst, bank[j][:], ACT.Identity, bias=self.ln_b[:],
                                             scale=self.ln_g[:]).then_inc(by_act, 1)

            @block.gpsimd
            def _(pool):
                for n in range(norms):
                    self.layernorm_pool(pool, s, n)

            @block.vector
            def _(dve):
                self.layernorm_dve(dve, self.x, xn, s, 0)
                if not causal:
                    dve.wait_ge(s["normed"], TILES)
                    self.layernorm_dve(dve, xn, xn, s, 1)
                for t in range(TILES):
                    dve.wait_ge(filled, TJ + t + 1)
                    src = bank[4 + t % 4][:, 0:3 * D]
                    if causal:
                        nc.vector.tensor_tensor(rows[:, t, :], src, bias[:], ALU.add).then_inc(by_dve, 1)
                    else:
                        b, tt = t // TPB, t % TPB
                        half = qkv[:, 4 * b:4 * b + 4].rearrange("p q (u t h) e -> p (q u) t h e", u=2, h=2)
                        for n in range(3):
                            cut = lambda v: v.rearrange("p (s u h e) -> p s u h e", s=3, h=2, e=HD)[:, n]
                            ins = nc.vector.tensor_tensor(half[:, :, tt, :, n * HD:(n + 1) * HD], cut(src),
                                                          cut(bias[:]), ALU.add)
                        ins.then_inc(by_dve, 1)

            @block.sync
            def _(sp):
                if causal:
                    per = TILES // QUADS
                    by_row = self.scratch_qkv.rearrange("(t p) f -> p t f", p=P)
                    by_pos = self.scratch_qkv.rearrange("r (c f) -> (r c) f", f=24) \
                                             .rearrange("(i n p) f -> p i n f", p=P, i=QUADS)
                    for i in range(QUADS):
                        sp.wait_ge(by_dve, per * (i + 1))
                        sp.dma_start(by_row[:, per * i:per * i + per, :], rows[:, per * i:per * i + per, :]) \
                          .then_inc(stored, 16)
                    for i in range(QUADS):
                        sp.wait_ge(stored, 16 * QUADS)
                        dst = qkv[:, i].rearrange("p (u t h) f -> p u h t f", u=2, h=2)
                        for g in range(4):
                            sp.dma_start(dst[:, g // 2, g % 2], by_pos[:, i, g * TPB:(g + 1) * TPB]).then_inc(back, 16)
                    sp.wait_ge(back, 16 * QUADS * 4)

    def attention(self, causal, qkv, y):
        nc = self.nc
        scale = 1.0 / (2.0 * D) ** 0.5 if causal else 1.0 / HD ** 0.5
        with ExitStack() as c:
            sb, sem = self.sb, self.sem
            q_stack = [sb(c, "q_stack", [P, 2, TPB, 2, STACK], BF16) for _ in range(2)]
            k_stack = [sb(c, "k_stack", [P, 2, TPB, 2, STACK], BF16) for _ in range(2)]
            v_aug = [sb(c, "v_aug", [P, 2, TPB, 2, 32]) for _ in range(2)]
            rest = sb(c, "rest", [P, 4 * TPB, HD])
            kt = [sb(c, "kt", [P, 2, SEQ], BF16) for _ in range(2)]
            qt_max = sb(c, "qt_max", [P, 2, SEQ], BF16)
            qt = [sb(c, "qt", [P, 2, SEQ], BF16) for _ in range(2)]
            mx = sb(c, "mx", [P, 2, TPB, 2])
            NP = 8
            probs = sb(c, "probs", [P, NP, BANK])
            ysum = sb(c, "ysum", [P, BANK])
            yrec = sb(c, "yrec", [P, 2, 4, 4])
            self.names += 1
            unit = [c.enter_context(nc.psum_tensor(f"unit{u}_{self.names}", [P, 2 * BANK], F32)) for u in range(2)]
            score = [c.enter_context(nc.psum_tensor(f"score{u}_{self.names}", [P, BANK], F32)) for u in range(3)]
            weighted = c.enter_context(nc.psum_tensor(f"weighted_{self.names}", [P, BANK], F32))

            blank, link, k_built, q_built, v_built = (sem(c, n) for n in ("blank", "link", "k_built", "q_built", "v_built"))
            unit_filled, unit_done = sem(c, "unit_filled"), sem(c, "unit_done")
            shift_link, shift_ready = sem(c, "shift_link"), sem(c, "shift_ready")
            scores_ready, probs_ready, probs_used = (sem(c, n) for n in ("scores_ready", "probs_ready", "probs_used"))
            sum_copied, norm_link = sem(c, "sum_copied"), sem(c, "norm_link")
            stored = sem(c, "stored")
            block = c.enter_context(nc.Block())

            SLOTS = [(qh, kb, max(0, kb * P - qh * BANK) if causal else 0) for qh in range(2) for kb in range(TPB)
                     if not causal or kb * P < (qh + 1) * BANK]
            NS = len(SLOTS)
            UNITS = 4 * NS
            HALF0 = sum(qh == 0 for qh, _, _ in SLOTS)
            diag = lambda qh, kb: causal and kb * P >= qh * BANK

            SPREAD = 0.94
            PREP = [("k", 0), ("q", 0), ("k", 1), ("q", 1)]
            PREP += [("max", 0, t, g) for t in range(TPB) for g in range(2)]
            PREP += [("max", 1, t, g) for t in range(2) for g in range(2)]
            PREP += [("shifted", 0)]
            PREP += [("max", 1, t, g) for t in range(2, TPB) for g in range(2)]
            PREP += [("shifted", 1)]
            NPREP = len(PREP)
            JOBS = NPREP + 2

            def columns(job):
                return {"max": 80 + ((job[2] + 1) * P if causal else SEQ) if job[0] == "max" else 0,
                        "y": 500}.get(job[0], 80 + SEQ // 2)

            def step_jobs(first, prep, last):
                by_place = [[] for _ in range(2 * NS + 1)]
                if prep:
                    jobs = PREP[:-1] + [("y", 0)] + PREP[-1:]
                    whole = sum(map(columns, jobs))
                    reach = sum(BANK - off for _, _, off in SLOTS)
                    ends, done = [], 0
                    for _, _, off in SLOTS:
                        for _ in range(2):
                            done += (BANK - off) / 2
                            ends.append(done / reach)
                    spent = 0
                    for job in jobs:
                        at = spent / whole * SPREAD
                        by_place[next(k for k, e in enumerate(ends) if e > at)].append(job)
                        spent += columns(job)
                else:
                    by_place[2 * (HALF0 + 2)].append(("y", 0))
                if not first:
                    by_place[4].insert(0, ("y", 1))
                if last:
                    by_place[2 * NS].append(("y", 1))
                return by_place

            def jobs_before(i):
                return NPREP if type(i) is int and i == 0 else JOBS * i + NPREP - 1

            def job_parity(i):
                return NPREP % 2 if type(i) is int and i == 0 else (NPREP - 1) % 2
            assert JOBS % 2 == 0

            def same_bank_before(u):
                if u >= 3:
                    return 3
                return next(UNITS - v for v in range(UNITS - 1, -1, -1) if v % 3 == u) + u

            def build(pool, i, par, links):
                n = [0]

                def chained(ins):
                    ins.then_inc(link, 1)
                    n[0] += 1
                    pool.wait_ge(link, links + n[0])

                if i >= 2:
                    pool.wait_ge(unit_filled, JOBS * i - 2 * JOBS + NPREP)
                for stack, off, his, mids, lo in ((k_stack[par], HD, (1, 4, 6), (2, 5), 3),
                                                  (q_stack[par], 0, (1, 2, 3), (4, 5), 6)):
                    src = qkv[:, i, :, off:off + HD]
                    part = lambda k: stack[:, :, :, :, 8 * k:8 * k + 8].rearrange("p u t h e -> p (u t h) e")
                    chained(nc.gpsimd.tensor_copy(part(his[0]), src))
                    for k in his[1:]:
                        nc.gpsimd.tensor_copy(part(k), part(his[0])).then_inc(link, 1)
                        n[0] += 1
                    chained(nc.gpsimd.tensor_tensor(rest[:], src, part(his[0]), ALU.subtract))
                    chained(nc.gpsimd.tensor_copy(part(mids[0]), rest[:]))
                    nc.gpsimd.tensor_copy(part(mids[1]), part(mids[0])).then_inc(link, 1)
                    n[0] += 1
                    chained(nc.gpsimd.tensor_tensor(rest[:], rest[:], part(mids[0]), ALU.subtract))
                    nc.gpsimd.tensor_copy(part(lo), rest[:]).then_inc(k_built if off else q_built, 1)
                    pool.wait_ge(k_built if off else q_built, i + 1)
                if i >= 2:
                    pool.wait_ge(probs_used, UNITS * i - UNITS)
                nc.gpsimd.tensor_copy(v_aug[par][:, :, :, :, 0:HD].rearrange("p u t h e -> p (u t h) e"),
                                      qkv[:, i, :, 2 * HD:3 * HD]) \
                  .then_inc(v_built, 1)
                return n[0]

            @block.gpsimd
            def _(pool):
                for b in range(2):
                    nc.gpsimd.memset(k_stack[b][:], 0.0).then_inc(blank, 1)
                    nc.gpsimd.memset(q_stack[b][:], 0.0).then_inc(blank, 1)
                    nc.gpsimd.memset(v_aug[b][:], 0.0).then_inc(blank, 1)
                pool.wait_ge(blank, 6)
                for b in range(2):
                    nc.gpsimd.memset(k_stack[b][:, :, :, :, 0:2], 1.0).then_inc(blank, 1)
                    nc.gpsimd.memset(v_aug[b][:, :, :, :, HD:HD + 1], 1.0).then_inc(blank, 1)
                pool.wait_ge(blank, 10)
                per = build(pool, 0, 0, 0)
                for i in range(1, QUADS):
                    build(pool, i, i % 2, i * per)

            def scores_of(pe, i, par, slot, first, heads):
                qh, kb, off = SLOTS[slot]
                for g in heads:
                    u = 4 * slot + g
                    back = same_bank_before(u)
                    if not (first and u < 3):
                        pe.wait_ge(probs_ready, i * UNITS + (u - back + 1))
                    rows = slice(64 * (g % 2), 64 * (g % 2) + STACK_USED)
                    out = score[u % 3]
                    ins = nc.tensor.matmul(out[:, off:BANK], kt[par][rows, g // 2, kb * P:kb * P + P],
                                           qt[par][rows, g // 2, qh * BANK + off:(qh + 1) * BANK],
                                           start=True, stop=not diag(qh, kb))
                    if diag(qh, kb):
                        ins = nc.tensor.matmul(out[:, off:off + P], self.identb[:], self.mask_kq[:],
                                               start=False, stop=True)
                    ins.then_inc(scores_ready, 1)

            def weigh(pe, i, par, slot, first):
                qh, kb, off = SLOTS[slot]
                if slot == 0:
                    pe.wait_ge(v_built, i + 1)
                    if not first:
                        pe.wait_ge(sum_copied, 2 * i)
                if slot == HALF0:
                    pe.wait_ge(sum_copied, 2 * i + 1)
                for g in range(4):
                    u = 4 * slot + g
                    pe.wait_ge(probs_ready, i * UNITS + u + 1)
                    nc.tensor.matmul(weighted[32 * g:32 * g + 32, off:BANK], v_aug[par][:, g // 2, kb, g % 2, :],
                                     probs[:, u % NP, off:BANK], start=kb == 0,
                                     stop=slot in (HALF0 - 1, NS - 1)).then_inc(probs_used, 1)

            def unit_job(pe, job, number, static_number, i_prep, par_prep, i):
                ubuf = unit[static_number % 2]
                if not (type(number) is int and number < 2):
                    pe.wait_ge(unit_done, number - 1)
                kind = job[0]
                if kind in ("k", "q", "shifted"):
                    pair = job[1]
                    if kind == "k":
                        pe.wait_ge(k_built, i_prep + 1)
                        src = k_stack[par_prep]
                    else:
                        src = q_stack[par_prep]
                        if kind == "q":
                            pe.wait_ge(q_built, i_prep + 1)
                        else:
                            pe.wait_ge(shift_ready, 2 * i_prep + pair + 1)
                    dst = ubuf[:].bitcast(BF16)
                    for t in range(TPB):
                        ins = nc.tensor.transpose(dst[:, t * P:(t + 1) * P], src[:, pair, t, :, :].rearrange("p h k -> p (h k)"),
                                                  self.identb[:])
                elif kind == "max":
                    _, pair, t, g = job
                    if t == 0 and g == 0:
                        pe.wait_ge(unit_done, number - max_since[pair])
                    rows = slice(64 * g, 64 * g + STACK_USED)
                    width = (t + 1) * P if causal else SEQ
                    for h in range(0, width, BANK):
                        end = min(h + BANK, width)
                        on_diag = causal and end == width
                        ins = nc.tensor.matmul(ubuf[:, h:end], qt_max[rows, pair, t * P:t * P + P],
                                               kt[par_prep][rows, pair, h:end], start=True, stop=not on_diag)
                        if on_diag:
                            ins = nc.tensor.matmul(ubuf[:, width - P:width], self.identb[:], self.mask_qk[:],
                                                   start=False, stop=True)
                else:
                    half = job[1]
                    pe.wait_ge(sum_copied, 2 * i + half + 1)
                    for t in range(4):
                        ins = nc.tensor.transpose(ubuf[:, t * P:(t + 1) * P], ysum[:, t * P:(t + 1) * P], self.ident[:])
                ins.then_inc(unit_filled, 1)

            max_since = {p: PREP.index(("max", p, 0, 0)) - PREP.index(("q", p)) - 1 for p in range(2)}

            def walk(i, first, prep, last):
                n = 0
                for place, jobs in enumerate(step_jobs(first, prep, last)):
                    for job in jobs:
                        quad = i + 1
                        if job[0] == "y":
                            quad = i - 1 if job[1] == 1 and place < 2 * NS else i
                        yield place, job, jobs_before(i) + n, job_parity(i) + n, quad
                        n += 1

            def pe_step(pe, i, par, first=False, prep=True, last=False):
                jobs = list(walk(i, first, prep, last))

                def jobs_at(place):
                    for at, job, number, static, quad in jobs:
                        if at == place:
                            unit_job(pe, job, number, static, quad, 1 - par, quad)

                pe.wait_ge(unit_done, jobs_before(i))
                for slot in range(NS):
                    scores_of(pe, i, par, slot, first, (0, 1))
                    jobs_at(2 * slot)
                    scores_of(pe, i, par, slot, first, (2, 3))
                    if slot:
                        weigh(pe, i, par, slot - 1, first)
                    elif not first:
                        weigh(pe, i - 1, 1 - par, NS - 1, False)
                    jobs_at(2 * slot + 1)
                if last:
                    weigh(pe, i, par, NS - 1, first)
                    jobs_at(2 * NS)

            def drive(engine, step):
                step(engine, 0, 0, first=True)
                with engine.Fori(1, QUADS - 1, 2) as i:
                    step(engine, i, 1)
                    step(engine, i + 1, 0)
                step(engine, QUADS - 1, 1, prep=False, last=True)

            @block.tensor
            def _(pe):
                pe.wait_ge(blank, 10)
                for n, job in enumerate(PREP):
                    unit_job(pe, job, n, n, 0, 0, 0)
                drive(pe, pe_step)

            flat = [job for jobs in step_jobs(False, True, False) for job in jobs]
            Y1_AT, Y0_AT = flat.index(("y", 1)), flat.index(("y", 0))

            def copy_sums(act, i, half, first=False, alone=False):
                act.wait_ge(probs_used, i * UNITS + (UNITS if half else 4 * HALF0))
                if half:
                    act.wait_ge(unit_filled, jobs_before(i) + 2 if alone else JOBS * i + NPREP + Y0_AT)
                elif not first:
                    act.wait_ge(unit_filled, jobs_before(i) + (0 if alone else Y1_AT) + 1)
                nc.scalar.activation(ysum[:], weighted[:], ACT.Copy).then_inc(sum_copied, 1)

            def act_step(act, i, par, first=False, prep=True, last=False):
                for slot in range(NS):
                    qh, kb, off = SLOTS[slot]
                    for g in range(4):
                        u = 4 * slot + g
                        act.wait_ge(scores_ready, i * UNITS + u + 1)
                        if not (first and u < NP):
                            act.wait_ge(probs_used, i * UNITS + (u - NP + 1))
                        nc.scalar.activation(probs[:, u % NP, off:BANK], score[u % 3][:, off:BANK], ACT.Exp,
                                             scale=scale).then_inc(probs_ready, 1)
                        if slot == 1 and g == 1 and not first:
                            copy_sums(act, i - 1, 1)
                        if slot == HALF0 + 1 and g == 1:
                            copy_sums(act, i, 0, first, not prep)
                if last:
                    copy_sums(act, i, 1, alone=True)

            @block.scalar
            def _(act):
                drive(act, act_step)

            def dve_job(dve, job, number, static_number, par_prep, quad, norms):
                ubuf = unit[static_number % 2]
                dve.wait_ge(unit_filled, number + 1)
                kind = job[0]
                if kind in ("k", "q", "shifted"):
                    pair = job[1]
                    dst = {"k": kt[par_prep], "q": qt_max, "shifted": qt[par_prep]}[kind]
                    nc.vector.tensor_copy(dst[:, pair, :], ubuf[:].bitcast(BF16)[:, 0:SEQ]).then_inc(unit_done, 1)
                elif kind == "max":
                    _, pair, t, g = job
                    width = (t + 1) * P if causal else SEQ
                    nc.vector.reduce_max(mx[:, pair, t, g:g + 1], ubuf[:, 0:width], AXX).then_inc(unit_done, 1)
                    if t == TPB - 1 and g == 1:
                        dve.wait_ge(unit_done, number + 1)
                        m = mx[:, pair].rearrange("p t h -> p (t h)")
                        hi = q_stack[par_prep][:, pair, :, :, 0].rearrange("p t h -> p (t h)")
                        lo = q_stack[par_prep][:, pair, :, :, 1].rearrange("p t h -> p (t h)")
                        nc.vector.tensor_scalar(hi, m, -1.0, None, ALU.mult).then_inc(shift_link, 1)
                        dve.wait_ge(shift_link, 2 * quad + pair + 1)
                        nc.vector.scalar_tensor_tensor(out=lo, in0=m, scalar=-1.0, in1=hi, op0=ALU.mult,
                                                       op1=ALU.subtract).then_inc(shift_ready, 1)
                else:
                    half = job[1]
                    sums = ubuf[:, 0:BANK].rearrange("p (t g e) -> p t g e", t=4, g=4)
                    nc.vector.reciprocal(yrec[:, half], sums[:, :, :, HD]).then_inc(norm_link, 1)
                    dve.wait_ge(norm_link, 2 * quad + half + 1)
                    dst = y[:, quad, 4 * half:4 * half + 4, :].rearrange("p t (g e) -> p t g e", g=4)
                    rec = yrec[:, half].unsqueeze(3).broadcast_to([P, 4, 4, HD])
                    nc.vector.tensor_tensor(dst, sums[:, :, :, 0:HD], rec, ALU.mult).then_inc(unit_done, 1)

            def dve_step(dve, i, par, first=False, prep=True, last=False):
                for s, job, number, static, quad in walk(i, first, prep, last):
                    dve_job(dve, job, number, static, 1 - par, quad, None)

            @block.vector
            def _(dve):
                for n, job in enumerate(PREP):
                    dve_job(dve, job, n, n, 0, 0, None)
                drive(dve, dve_step)

            total = JOBS * QUADS
            @block.sync
            def _(sp):
                if causal:
                    sp.wait_ge(unit_done, total)
                    dst = self.scratch_y.rearrange("(n p e) -> p n e", p=P, e=HD)
                    for i in range(QUADS):
                        for t in range(TPB):
                            sp.dma_start(dst[:, i * 32:(i + 1) * 32, :].rearrange("p (g t) e -> p t g e", g=4)[:, t],
                                         y[:, i, t, :].rearrange("p (g e) -> p g e", g=4)).then_inc(stored, 16)
                    sp.wait_ge(stored, 16 * QUADS * TPB)

    def residual(self, causal, y):
        nc = self.nc
        with ExitStack() as c:
            rows = self.sb(c, "yrows", [P, TILES, D])
            back, added = self.sem(c, "back"), self.sem(c, "added")
            block = c.enter_context(nc.Block())

            @block.sync
            def _(sp):
                if causal:
                    sp.dma_start(rows[:], self.scratch_y.rearrange("(t p d) -> p t d", p=P, d=D)).then_inc(back, 16)

            @block.vector
            def _(dve):
                if causal:
                    dve.wait_ge(back, 16)
                    nc.vector.tensor_tensor(self.x[:], self.x[:], rows[:], ALU.add).then_inc(added, 1)
                else:
                    for b in range(BATCH):
                        xv = self.x[:, b * TPB:(b + 1) * TPB, :].rearrange("p t (q e) -> p q t e", q=4)
                        nc.vector.tensor_tensor(xv, xv, y[:, 4 * b:4 * b + 4], ALU.add).then_inc(added, 1)

    def mixture(self, final):
        nc = self.nc
        NT = 16
        with ExitStack() as c:
            sb, sem = self.sb, self.sem
            mid = sb(c, "mid", [P, 8, BANK])
            xn = mid[:, 0:4, :].rearrange("p q (t d) -> p (q t) d", t=4)
            xt = mid[:, 4:8, :].rearrange("p q (t r) -> p (q t) r", t=4)
            tok = sb(c, "tok", [P, 4, NT, D1])
            fa = sb(c, "fa", [P, 8192])
            fb = sb(c, "fb", [P, 8192])
            hid = sb(c, "hid", [P, P, F1])
            logit = sb(c, "logit", [P, 2, EXPERTS])
            top = sb(c, "top", [P, 2, 8])
            index = sb(c, "index", [P, 2, 8], U32)
            indexf = sb(c, "indexf", [P, 2, 2])
            gap = sb(c, "gap", [P, 2, 4])
            onehot = sb(c, "onehot", [P, 2, 4, EXPERTS])
            pick = sb(c, "pick", [EXPERTS, 2, 512])
            yt = tok[:].rearrange("p q t i -> p q (t i)")
            s = self.layernorm_state(c)
            bank = self.banks(c)
            filled, by_dve, by_act = sem(c, "filled"), sem(c, "by_dve"), sem(c, "by_act")
            top_link, gap_ready, exp_ready, gelu_done = (sem(c, n) for n in ("top_link", "gap_ready", "exp_ready", "gelu_done"))
            stored = sem(c, "stored")
            block = c.enter_context(nc.Block())

            ROUTED = 11

            JOBS = [("xt", j) for j in range(4)] + [("tok", j) for j in range(4)]
            JOBS += [("route_up", n) for n in range(2)] + [("pick_up", n) for n in range(2)]
            JOBS += [("fetch_up", w, j) for w in range(2) for j in range(16)]
            for r in range(8):
                JOBS += [("first_up", 2 * r), ("first_up", 2 * r + 1), ("second_up", r, 0), ("second_up", r, 1)]
            JOBS += [("route_down", n) for n in range(2)] + [("pick_down", n) for n in range(2)]
            JOBS += [("fetch_down", w, j) for w in range(2) for j in range(16)]
            for q in range(4):
                JOBS += [("first_down", q, g2, j) for g2 in range(2) for j in range(2)] + [("second_down", q)]
            JOBS += [("back", g) for g in range(4)]
            BY_TURNS = {"xt", "tok", "fetch_up", "fetch_down", "first_up", "first_down"}
            on_act = [n % 2 == 1 and job[0] in BY_TURNS for n, job in enumerate(JOBS)]
            number = {job: n for n, job in enumerate(JOBS)}

            def emptied(eng, job):
                n = number[job]
                if on_act[n]:
                    eng.wait_ge(by_act, sum(on_act[:n + 1]))
                else:
                    eng.wait_ge(by_dve, n + 1 - sum(on_act[:n + 1]))

            def bank_free(pe, n):
                if n >= 8:
                    emptied(pe, JOBS[n - 8])

            def all_emptied(eng, jobs):
                for who in (False, True):
                    of = [j for j in jobs if on_act[number[j]] == who]
                    if of:
                        emptied(eng, max(of, key=number.get))

            @block.tensor
            def _(pe):
                for n, job in enumerate(JOBS):
                    b = bank[n % 8]
                    kind = job[0]
                    if kind == "route_down" and job[1] == 1:
                        continue
                    bank_free(pe, n)
                    if kind == "xt":
                        for t in range(4 * job[1], 4 * job[1] + 4):
                            pe.wait_ge(s["normed"], t + 1)
                            ins = nc.tensor.transpose(b[:, (t % 4) * P:(t % 4 + 1) * P], xn[:, t, :], self.ident[:])
                    elif kind == "tok":
                        for g in range(4):
                            for c4 in range(4):
                                ins = nc.tensor.matmul(b[32 * g:32 * g + 32, c4 * P:(c4 + 1) * P],
                                                       xn[:, 4 * job[1] + g, 32 * c4:32 * c4 + 32], self.ident[:],
                                                       start=True, stop=True)
                    elif kind == "route_up":
                        all_emptied(pe, [("xt", j) for j in range(4)])
                        v = xt[:, 8 * job[1]:8 * job[1] + 8, :].rearrange("c t (n r) -> c (t n) r", r=TOKROWS)
                        for r in range(TOKROWS):
                            ins = nc.tensor.matmul(b[:, 0:EXPERTS], v[:, :, r], self.router_up[:, r, :],
                                                   start=r == 0, stop=r == TOKROWS - 1)
                    elif kind in ("pick_up", "pick_down"):
                        layer = kind == "pick_down"
                        pe.wait_ge(top_link, ROUTED * (2 * layer + job[1] + 1))
                        for k in range(4):
                            ins = nc.tensor.transpose(b[0:EXPERTS, k * P:(k + 1) * P], onehot[:, job[1], k, :],
                                                      self.ident[:])
                    elif kind == "fetch_up":
                        _, w, j = job
                        if w == 0 and j == 0:
                            emptied(pe, ("pick_up", 1))
                        table = self.tab["B_up" if w else "A_up"]
                        for o in range(4):
                            for g in range(4):
                                ins = nc.tensor.matmul(b[32 * g:32 * g + 32, o * P:(o + 1) * P],
                                                       table[:, (4 * j + o) * D1:(4 * j + o + 1) * D1],
                                                       pick[:, w, g * P:(g + 1) * P], start=True, stop=True)
                    elif kind == "first_up":
                        j = job[1]
                        if j == 0:
                            all_emptied(pe, [("tok", q) for q in range(4)])
                            all_emptied(pe, [("fetch_up", w, k) for w in range(2) for k in range(16)])
                        for t in range(4):
                            n_tok = 4 * j + t
                            for g in range(4):
                                rows = slice(32 * g, 32 * g + 32)
                                ins = nc.tensor.matmul(b[rows, t * P:(t + 1) * P], tok[rows, n_tok // NT, n_tok % NT, :],
                                                       fb[rows, n_tok * P:(n_tok + 1) * P], start=True, stop=True)
                    elif kind == "second_up":
                        _, r, g2 = job
                        emptied(pe, ("first_up", 2 * r))
                        emptied(pe, ("first_up", 2 * r + 1))
                        for t in range(8):
                            n_tok = 8 * r + t
                            m = mid[:, (2 * r + t // 4) % 8, :]
                            for half in range(2):
                                g = 2 * g2 + half
                                rows = slice(32 * g, 32 * g + 32)
                                for k in range(2):
                                    at = (t % 4) * P + k * F1
                                    ins = nc.tensor.matmul(b[64 * half:64 * half + 64, t * F1:(t + 1) * F1],
                                                           m[rows, at:at + F1],
                                                           fa[rows, n_tok * P + k * F1:n_tok * P + (k + 1) * F1],
                                                           start=k == 0, stop=k == 1)
                    elif kind == "route_down":
                        bank_free(pe, n + 1)
                        pe.wait_ge(gelu_done, 16)
                        for o in range(F1):
                            for half in range(2):
                                rows = slice(64 * half, 64 * half + 64)
                                ins = nc.tensor.matmul(bank[(n + half) % 8][:, 0:EXPERTS], hid[rows, :, o],
                                                       self.router_dn[rows, o, :], start=o == 0, stop=o == F1 - 1)
                                if o == F1 - 1 and half == 0:
                                    ins.then_inc(filled, 1)
                    elif kind == "fetch_down":
                        _, w, j = job
                        if w == 0 and j == 0:
                            emptied(pe, ("pick_down", 1))
                        table = self.tab["B_down" if w else "A_down"]
                        for o in range(2):
                            for half in range(2):
                                ins = nc.tensor.matmul(b[64 * half:64 * half + 64, o * 256:(o + 1) * 256],
                                                       table[:, (2 * j + o) * F1:(2 * j + o + 1) * F1],
                                                       pick[:, w, half * 256:(half + 1) * 256], start=True, stop=True)
                    elif kind == "first_down":
                        _, q, g2, j = job
                        if (q, g2, j) == (0, 0, 0):
                            all_emptied(pe, [("fetch_down", w, k) for w in range(2) for k in range(16)])
                        for t in range(8):
                            n_tok = g2 * 64 + q * NT + 8 * j + t
                            for half in range(2):
                                rows = slice(64 * half, 64 * half + 64)
                                ins = nc.tensor.matmul(b[rows, t * 64:(t + 1) * 64], hid[rows, n_tok, :],
                                                       fb[rows, n_tok * 64:(n_tok + 1) * 64], start=True, stop=True)
                    elif kind == "second_down":
                        q = job[1]
                        all_emptied(pe, [("first_down", q, g2, j) for g2 in range(2) for j in range(2)])
                        for t in range(NT):
                            for g2 in range(2):
                                n_tok = g2 * 64 + q * NT + t
                                m = mid[:, (4 * q + 2 * g2 + t // 8) % 8, :]
                                for half in range(2):
                                    g = 2 * g2 + half
                                    rows = slice(64 * half, 64 * half + 64)
                                    for k in range(2):
                                        at = (t % 8) * 64 + k * D1
                                        ins = nc.tensor.matmul(b[32 * g:32 * g + 32, t * D1:(t + 1) * D1],
                                                               m[rows, at:at + D1],
                                                               fa[rows, n_tok * 64 + k * D1:n_tok * 64 + (k + 1) * D1],
                                                               start=k == 0, stop=k == 1)
                    elif kind == "back":
                        g = job[1]
                        rows = slice(32 * g, 32 * g + 32)
                        if g == 0:
                            emptied(pe, ("second_down", 3))
                        for q in range(4):
                            v = yt[:, q].rearrange("p (r c) -> p r c", c=4)
                            for c4 in range(4):
                                ins = nc.tensor.transpose(b[:, q * P + c4 * D1:q * P + (c4 + 1) * D1], v[rows, :, c4],
                                                          self.ident[rows, rows])
                    ins.then_inc(filled, 1)

            def route(dve, b, layer, n):
                base = ROUTED * (2 * layer + n)
                count = [0]

                def link(ins):
                    count[0] += 1
                    ins.then_inc(top_link, 1)
                    dve.wait_ge(top_link, base + count[0])

                lg, tp, gp = logit[:, n, :], top[:, n, :], gap[:, n, :]
                nc.vector.tensor_copy(lg, b[:, 0:EXPERTS]).then_inc(by_dve, 1)
                dve.wait_ge(by_dve, dve_count[0] + 1)
                link(nc.vector.max(tp, lg))
                link(nc.vector.max_index(index[:, n, :], tp, lg))
                link(nc.vector.tensor_copy(indexf[:, n, :], index[:, n, 0:2]))
                link(nc.vector.tensor_tensor(gp[:, 0:1], tp[:, 1:2], tp[:, 0:1], ALU.subtract))
                dve.wait_ge(exp_ready, 2 * layer + n + 1)
                link(nc.vector.tensor_scalar(gp[:, 2:3], gp[:, 1:2], 1.0, None, ALU.add))
                link(nc.vector.reciprocal(gp[:, 2:3], gp[:, 2:3]))
                link(nc.vector.tensor_tensor(gp[:, 3:4], gp[:, 1:2], gp[:, 2:3], ALU.mult))
                for k in range(2):
                    nc.vector.tensor_scalar(onehot[:, n, k, :], self.iota_e[:], indexf[:, n, k:k + 1],
                                            gp[:, 2 + k:3 + k], ALU.is_equal, ALU.mult).then_inc(top_link, 1)
                    nc.vector.tensor_scalar(onehot[:, n, 2 + k, :], self.iota_e[:], indexf[:, n, k:k + 1],
                                            None, ALU.is_equal).then_inc(top_link, 1)
                    count[0] += 2
                assert count[0] == ROUTED

            def moves(job, b):
                kind = job[0]
                if kind == "xt":
                    return [(xt[:, 4 * job[1]:4 * job[1] + 4, :].rearrange("p t r -> p (t r)"), b[:])]
                if kind == "tok":
                    return [(tok[:, job[1], :, :].rearrange("p t (r c) -> p c (t r)", c=4),
                             b[:].rearrange("p (c r) -> p c r", c=4))]
                if kind == "fetch_up":
                    _, w, j = job
                    f = fb if w else fa
                    return [(f[:].rearrange("p (n o) -> p o n", o=F1)[:, 4 * j:4 * j + 4, :],
                             b[:].rearrange("p (o n) -> p o n", o=4))]
                if kind == "fetch_down":
                    _, w, j = job
                    f = fb if w else fa
                    return [(f[:].rearrange("p (n o) -> p o n", o=D1)[:, 2 * j:2 * j + 2, :],
                             b[:].rearrange("p (o n) -> p o n", o=2))]
                if kind == "first_up":
                    return [(mid[:, job[1] % 8, :], b[:])]
                _, q, g2, j = job
                return [(mid[:, (4 * q + 2 * g2 + j) % 8, :], b[:])]

            dve_count = [0]

            @block.vector
            def _(dve):
                self.layernorm_dve(dve, self.x, xn, s, 0)
                for n, job in enumerate(JOBS):
                    if on_act[n]:
                        continue
                    b = bank[n % 8]
                    kind = job[0]
                    dve.wait_ge(filled, n + 1)
                    if kind in BY_TURNS:
                        for dst, src in moves(job, b):
                            nc.vector.tensor_copy(dst, src).then_inc(by_dve, 1)
                    elif kind == "route_up":
                        route(dve, b, 0, job[1])
                    elif kind == "route_down":
                        route(dve, b, 1, job[1])
                    elif kind == "pick_up":
                        for k in range(4):
                            v = pick[:, k // 2, :].rearrange("e (g q t k) -> e q g t k", g=4, q=4, k=2)
                            ins = nc.vector.tensor_copy(v[:, 2 * job[1]:2 * job[1] + 2, :, :, k % 2],
                                                        b[0:EXPERTS, k * P:(k + 1) * P]
                                                        .rearrange("e (q g t) -> e q g t", q=2, g=4))
                        ins.then_inc(by_dve, 1)
                    elif kind == "pick_down":
                        for k in range(4):
                            v = pick[:, k // 2, :].rearrange("e (h t k) -> e h t k", h=2, k=2)
                            ins = nc.vector.tensor_copy(v[:, job[1], :, k % 2], b[0:EXPERTS, k * P:(k + 1) * P])
                        ins.then_inc(by_dve, 1)
                    elif kind == "second_up":
                        _, r, g2 = job
                        dst = hid[:, g2 * 64 + 8 * r:g2 * 64 + 8 * r + 8, :]
                        bias = self.bias_up[:].unsqueeze(1).broadcast_to([P, 8, F1])
                        nc.vector.scalar_tensor_tensor(out=dst, in0=b[:].rearrange("p (t o) -> p t o", t=8),
                                                       scalar=self.scale_up[:], in1=bias, op0=ALU.mult,
                                                       op1=ALU.add).then_inc(by_dve, 1)
                    elif kind == "second_down":
                        bias = self.bias_dn[:].unsqueeze(1).broadcast_to([P, NT, D1])
                        nc.vector.scalar_tensor_tensor(out=yt[:, job[1]].rearrange("p (t o) -> p t o", t=NT),
                                                       in0=b[:].rearrange("p (t o) -> p t o", t=NT),
                                                       scalar=self.scale_dn[:], in1=bias, op0=ALU.mult,
                                                       op1=ALU.add).then_inc(by_dve, 1)
                    elif kind == "back":
                        xv = self.x[:].rearrange("p (q g) d -> p g q d", g=4)[:, job[1]]
                        nc.vector.tensor_tensor(xv, b[:].rearrange("p (q d) -> p q d", q=4), xv, ALU.add) \
                          .then_inc(by_dve, 1)
                    dve_count[0] += 1

            @block.scalar
            def _(act):
                for n, job in enumerate(JOBS):
                    b = bank[n % 8]
                    if on_act[n]:
                        act.wait_ge(filled, n + 1)
                        for dst, src in moves(job, b):
                            nc.scalar.activation(dst, src, ACT.Copy).then_inc(by_act, 1)
                    elif job[0] in ("route_up", "route_down"):
                        r = 2 * (job[0] == "route_down") + job[1]
                        act.wait_ge(top_link, ROUTED * r + 4)
                        nc.scalar.activation(gap[:, job[1], 1:2], gap[:, job[1], 0:1], ACT.Exp).then_inc(exp_ready, 1)
                    elif job[0] == "second_up":
                        _, r, g2 = job
                        emptied(act, job)
                        v = hid[:, g2 * 64 + 8 * r:g2 * 64 + 8 * r + 8, :]
                        nc.scalar.activation(v, v, ACT.Gelu).then_inc(gelu_done, 1)

            @block.gpsimd
            def _(pool):
                self.layernorm_pool(pool, s, 0)

            @block.sync
            def _(sp):
                if final:
                    emptied(sp, ("back", 3))
                    sp.dma_start(self.out.rearrange("b (t p) d -> p (b t) d", p=P), self.x[:]).then_inc(stored, 16)
                    sp.wait_ge(stored, 16)

    def build(self):
        nc = self.nc
        self.scratch_qkv = nc.dram_tensor("scratch_qkv", [BATCH * SEQ, 3 * D], F32, kind="Internal").ap()
        self.scratch_y = nc.dram_tensor("scratch_y", [BATCH * SEQ * D], F32, kind="Internal").ap()
        with ExitStack() as ctx:
            self.setup(ctx)
            for causal in (False, True):
                with ExitStack() as c:
                    y = self.sb(c, "y", [P, QUADS, TPB, 32])
                    with ExitStack() as c2:
                        qkv = self.sb(c2, "qkv", [P, QUADS, 4 * TPB, 24])
                        self.project(causal, qkv)
                        self.attention(causal, qkv, y)
                    self.residual(causal, y)
                self.mixture(final=causal)


_INS = ["L0_attn_a_x", "L0_attn_a_ln_g", "L0_attn_a_ln_b", "L0_attn_a_Wq", "L0_attn_a_bq", "L0_attn_a_Wk",
        "L0_attn_a_bk", "L0_attn_a_Wv", "L0_attn_a_bv", "L0_attn_b_qkv_kernel", "L0_attn_b_qkv_bias",
        "L0_ffn_W_up", "L0_ffn_A_up", "L0_ffn_B_up", "L0_ffn_scale_up", "L0_ffn_bias_up", "L0_ffn_W_down",
        "L0_ffn_A_down", "L0_ffn_B_down", "L0_ffn_scale_down", "L0_ffn_bias_down"]


def kernel(**inputs):
    import numpy as _np
    import concourse.bacc as _bacc
    from concourse import mybir as _mybir
    from concourse.bass_utils import run_bass_kernel_spmd as _run

    nc = _bacc.Bacc("TRN2", target_bir_lowering=False, num_devices=1)
    arrays, aps = {}, {}
    for name in _INS:
        a = _np.ascontiguousarray(inputs[name])
        arrays[f"in_{name}"] = a
        aps[name] = nc.dram_tensor(f"in_{name}", a.shape, _mybir.dt.from_np(a.dtype), kind="ExternalInput").ap()
    out = nc.dram_tensor("out_0", (BATCH, SEQ, D), F32, kind="ExternalOutput").ap()
    Kernel(nc, aps, out).build()
    r = _run(nc, [arrays], core_ids=[0])
    return r.results[0]["out_0"]
```

```python
from contextlib import ExitStack

import concourse.bass as bass
from concourse import mybir

F32 = mybir.dt.float32
BF16 = mybir.dt.bfloat16
U32 = mybir.dt.uint32
ALU = mybir.AluOpType
ACT = mybir.ActivationFunctionType
AXX = mybir.AxisListType.X

P = 128
BATCH, SEQ, D = 2, 1024, 128
HEADS, HD = 16, 8
TILES = BATCH * SEQ // P
TPB = SEQ // P
QUADS = BATCH * HEADS // 4
EXPERTS = 64
D1, F1 = 32, 64
TOKROWS = D1 * D1 // D
EPS = 1e-5
MASKED = -1e30
TABLES = ("A_up", "B_up", "A_down", "B_down")
BANK = 512
STACK = 64
ROUTED = 17
STACK_USED = 56


class Kernel:
    def __init__(self, nc, a, out):
        self.nc, self.a, self.out = nc, a, out
        self.names = 0

    def sem(self, ctx, name):
        self.names += 1
        return ctx.enter_context(self.nc.semaphore(f"{name}_{self.names}"))

    def sb(self, ctx, name, shape, dt=F32):
        self.names += 1
        return ctx.enter_context(self.nc.sbuf_tensor(f"{name}_{self.names}", shape, dt))

    def banks(self, ctx, n=8):
        self.names += 1
        return [ctx.enter_context(self.nc.psum_tensor(f"bank{i}_{self.names}", [P, BANK], F32)) for i in range(n)]

    def setup(self, ctx):
        nc, a = self.nc, self.a
        sb = self.sb
        self.x = sb(ctx, "x", [P, TILES, D])
        self.ident = sb(ctx, "ident", [P, P])
        self.identb = sb(ctx, "identb", [P, P], BF16)
        self.mask_qk = sb(ctx, "mask_qk", [P, P], BF16)
        self.mask_kq = sb(ctx, "mask_kq", [P, P], BF16)
        self.half_neg = sb(ctx, "half_neg", [P, TILES])
        self.iota_e = sb(ctx, "iota_e", [P, 2 * EXPERTS])
        self.ones = sb(ctx, "ones", [EXPERTS, 64])
        self.w_qkv = sb(ctx, "w_qkv", [P, 3 * D])
        self.w_qkv_b = sb(ctx, "w_qkv_b", [P, 3 * D])
        self.b_qkv = sb(ctx, "b_qkv", [P, 3 * D])
        self.b_qkv_b = sb(ctx, "b_qkv_b", [P, 3 * D])
        self.ln_g = sb(ctx, "ln_g", [P, 1])
        self.ln_b = sb(ctx, "ln_b", [P, 1])
        self.router_up = sb(ctx, "router_up", [P, TOKROWS, EXPERTS])
        self.router_dn = sb(ctx, "router_dn", [P, F1, EXPERTS])
        self.tab_hm = {k: sb(ctx, k + "_hm", [P, F1 * D1], BF16) for k in TABLES}
        self.tab_lo = {k: sb(ctx, k + "_lo", [P, F1 * D1], BF16) for k in TABLES}
        self.bias_up = sb(ctx, "bias_up", [P, F1])
        self.bias_dn = sb(ctx, "bias_dn", [P, D1])
        self.scale_up = sb(ctx, "scale_up", [P, 1])
        self.scale_dn = sb(ctx, "scale_dn", [P, 1])

        with ExitStack() as c:
            wu = sb(c, "wu", [EXPERTS, D1 * D1])
            wd = sb(c, "wd", [EXPERTS, F1 * F1])
            bd = sb(c, "bd", [D1, D1])
            whole = {k: sb(c, k, [EXPERTS, F1 * D1]) for k in TABLES}
            mid = [sb(c, "mid", [EXPERTS, F1 * D1], BF16) for _ in range(2)]
            bank = self.banks(c)
            x_in, loaded, chain, const = (self.sem(c, n) for n in ("x_in", "loaded", "chain", "const"))
            filled, evacuated = self.sem(c, "filled"), self.sem(c, "evacuated")
            tables_in = [self.sem(c, "table_in") for _ in TABLES]
            high_done, rest_done, mid_done, low_done = (
                self.sem(c, n) for n in ("high_done", "rest_done", "mid_done", "low_done"))
            mid_moved = [self.sem(c, "mid_moved") for _ in range(2)]
            block = c.enter_context(nc.Block())
            JOBS = 1 + F1 // 8 + 1

            @block.sync
            def _(sp):
                sp.dma_start(wd[:], a["L0_ffn_W_down"]).then_inc(loaded, 16)
                sp.dma_start(wu[:], a["L0_ffn_W_up"]).then_inc(loaded, 16)
                sp.dma_start(bd[:], a["L0_ffn_bias_down"].rearrange("(o p) -> o p", p=D1)).then_inc(loaded, 16)
                for n, k in enumerate(TABLES):
                    sp.dma_start(whole[k][:], a["L0_ffn_" + k].rearrange("e o i -> e (o i)")).then_inc(tables_in[n], 16)
                sp.dma_start(self.x[:], a["L0_attn_a_x"].rearrange("b (t p) d -> p (b t) d", p=P)).then_inc(x_in, 16)
                for n, k in enumerate(("Wq", "Wk", "Wv")):
                    sp.dma_start(self.w_qkv[:, n * D:(n + 1) * D], a["L0_attn_a_" + k]).then_inc(x_in, 16)
                sp.dma_start(self.w_qkv_b[:], a["L0_attn_b_qkv_kernel"]).then_inc(x_in, 16)
                for n, k in enumerate(TABLES):
                    sp.wait_ge(mid_done, n + 1)
                    sp.dma_start(self.tab_hm[k][EXPERTS:P, :], mid[n % 2][:]).then_inc(mid_moved[n % 2], 16)
                sp.wait_ge(x_in, 5 * 16)
                for n in range(2):
                    sp.wait_ge(mid_moved[n], 2 * 16)

            @block.scalar
            def _(act):
                for n, k in enumerate(("bq", "bk", "bv")):
                    act.dma_start(self.b_qkv[:, n * D:(n + 1) * D],
                                  a["L0_attn_a_" + k].partition_broadcast(P)).then_inc(const, 16)
                act.dma_start(self.b_qkv_b[:], a["L0_attn_b_qkv_bias"][0].partition_broadcast(P)).then_inc(const, 16)
                act.dma_start(self.ln_g[:], a["L0_attn_a_ln_g"].rearrange("(p o) -> p o", o=1)).then_inc(const, 16)
                act.dma_start(self.ln_b[:], a["L0_attn_a_ln_b"].rearrange("(p o) -> p o", o=1)).then_inc(const, 16)
                act.dma_start(self.scale_up[:], a["L0_ffn_scale_up"].partition_broadcast(P)).then_inc(const, 16)
                act.dma_start(self.scale_dn[:], a["L0_ffn_scale_down"].partition_broadcast(P)).then_inc(const, 16)
                for half in range(2):
                    act.dma_start(self.bias_up[64 * half:64 * half + 64, :],
                                  a["L0_ffn_bias_up"].rearrange("(o p) -> o p", p=F1)).then_inc(const, 16)
                for n, k in enumerate(TABLES):
                    act.wait_ge(tables_in[n], 16)
                    nc.scalar.activation(self.tab_hm[k][0:EXPERTS, :], whole[k][:], ACT.Copy).then_inc(high_done, 1)
                    act.wait_ge(rest_done, n + 1)
                    if n >= 2:
                        act.wait_ge(mid_moved[n % 2], 16)
                        act.wait_ge(low_done, n - 1)
                    nc.scalar.activation(mid[n % 2][:], whole[k][:], ACT.Copy).then_inc(mid_done, 1)
                act.wait_ge(const, 10 * 16)

            @block.gpsimd
            def _(pool):
                nc.gpsimd.memset(self.ident[:], 0.0).then_inc(chain, 1)
                nc.gpsimd.memset(self.identb[:], 0.0).then_inc(chain, 1)
                nc.gpsimd.memset(self.mask_qk[:], 0.0).then_inc(chain, 1)
                nc.gpsimd.memset(self.mask_kq[:], 0.0).then_inc(chain, 1)
                nc.gpsimd.memset(self.half_neg[:], -0.5).then_inc(chain, 1)
                nc.gpsimd.iota(self.iota_e[:], pattern=[[0, 2], [1, EXPERTS]], base=0, channel_multiplier=0,
                               allow_small_or_imprecise_dtypes=True).then_inc(chain, 1)
                pool.wait_ge(chain, 6)
                for m in (self.ident, self.identb):
                    nc.gpsimd.affine_select(out=m[:], in_=m[:], pattern=[[-1, P]], compare_op=ALU.not_equal,
                                            fill=1.0, base=0, channel_multiplier=1).then_inc(chain, 1)
                nc.gpsimd.affine_select(out=self.mask_qk[:], in_=self.mask_qk[:], pattern=[[-1, P]],
                                        compare_op=ALU.is_ge, fill=MASKED, base=0,
                                        channel_multiplier=1).then_inc(chain, 1)
                nc.gpsimd.affine_select(out=self.mask_kq[:], in_=self.mask_kq[:], pattern=[[1, P]],
                                        compare_op=ALU.is_ge, fill=MASKED, base=0,
                                        channel_multiplier=-1).then_inc(chain, 1)
                nc.gpsimd.memset(self.ones[:], 1.0).then_inc(chain, 1)
                pool.wait_ge(chain, 11)
                for k in TABLES:
                    nc.gpsimd.memset(self.tab_lo[k][EXPERTS:P, :], 0.0).then_inc(chain, 1)

            @block.tensor
            def _(pe):
                pe.wait_ge(chain, 10)
                pe.wait_ge(loaded, 3 * 16)
                for r in range(TOKROWS):
                    last = nc.tensor.transpose(bank[0][:, r * 64:(r + 1) * 64], wu[:, r * D:(r + 1) * D],
                                               self.ident[0:64, 0:64])
                last.then_inc(filled, 1)
                wd_by_p = wd[:].rearrange("e (o p) -> e p o", p=F1)
                for j in range(F1 // 8):
                    if j == 7:
                        pe.wait_ge(evacuated, 1)
                    for p in range(8):
                        for half in range(2):
                            last = nc.tensor.matmul(bank[(1 + j) % 8][64 * half:64 * half + 64, p * 64:(p + 1) * 64],
                                                    wd_by_p[:, 8 * j + p, :], self.ident[0:64, 0:64],
                                                    start=True, stop=True)
                    last.then_inc(filled, 1)
                pe.wait_ge(evacuated, 2)
                for g in range(4):
                    last = nc.tensor.matmul(bank[1][32 * g:32 * g + 32, 0:D1], bd[:], self.ident[0:32, 0:32],
                                            start=True, stop=True)
                last.then_inc(filled, 1)

            @block.vector
            def _(dve):
                def empty(j):
                    dve.wait_ge(filled, j + 1)
                    b = bank[j % 8]
                    if j == 0:
                        nc.vector.tensor_copy(self.router_up[:].rearrange("p r e -> p (r e)"), b[:]).then_inc(evacuated, 1)
                    elif j < JOBS - 1:
                        nc.vector.tensor_copy(self.router_dn[:, 8 * (j - 1):8 * j, :].rearrange("p o e -> p (o e)"),
                                              b[:]).then_inc(evacuated, 1)
                    else:
                        nc.vector.tensor_copy(self.bias_dn[:], b[:, 0:D1]).then_inc(evacuated, 1)

                for n, k in enumerate(TABLES):
                    dve.wait_ge(high_done, n + 1)
                    nc.vector.tensor_tensor(whole[k][:], whole[k][:], self.tab_hm[k][0:EXPERTS, :],
                                            ALU.subtract).then_inc(rest_done, 1)
                    empty(2 * n)
                    empty(2 * n + 1)
                    dve.wait_ge(mid_done, n + 1)
                    nc.vector.tensor_tensor(self.tab_lo[k][0:EXPERTS, :], whole[k][:], mid[n % 2][:],
                                            ALU.subtract).then_inc(low_done, 1)
                empty(JOBS - 2)
                empty(JOBS - 1)

    def layernorm_dve(self, dve, src, dst, s, tag):
        nc = self.nc
        for t in range(TILES):
            nc.vector.bn_stats(s["stats"][:, t, :], src[:, t, :]).then_inc(s["stat_done"], 1)
        dve.wait_ge(s["stat_done"], (2 * tag + 1) * TILES)
        for t in range(TILES):
            nc.vector.bn_aggr(s["meanvar"][:, t, :], s["stats"][:, t, :]).then_inc(s["stat_done"], 1)
        dve.wait_ge(s["rstd_done"], 2 * tag + 2)
        for t in range(TILES):
            nc.vector.tensor_scalar(dst[:, t, :], src[:, t, :], s["meanvar"][:, t, 0:1], s["rstd"][:, t:t + 1],
                                    ALU.subtract, ALU.mult).then_inc(s["normed"], 1)

    def layernorm_pool(self, pool, s, tag):
        nc = self.nc
        pool.wait_ge(s["stat_done"], (2 * tag + 2) * TILES)
        nc.gpsimd.tensor_scalar(s["rstd"][:], s["meanvar"][:, :, 1], EPS, None, ALU.add).then_inc(s["rstd_done"], 1)
        pool.wait_ge(s["rstd_done"], 2 * tag + 1)
        nc.gpsimd.tensor_tensor(s["rstd"][:], s["rstd"][:], self.half_neg[:], ALU.pow).then_inc(s["rstd_done"], 1)

    def layernorm_state(self, c):
        s = {n: self.sem(c, n) for n in ("stat_done", "rstd_done", "normed")}
        s["stats"] = self.sb(c, "stats", [P, TILES, 6])
        s["meanvar"] = self.sb(c, "meanvar", [P, TILES, 2])
        s["rstd"] = self.sb(c, "rstd", [P, TILES])
        return s

    def project(self, causal, qkv):
        nc = self.nc
        with ExitStack() as c:
            xn = self.sb(c, "xn", [P, TILES, D])
            xt = self.sb(c, "xt", [P, TILES, P])
            rows = self.sb(c, "rows", [P, TILES, 3 * D]) if causal else None
            s = self.layernorm_state(c)
            bank = self.banks(c)
            filled, by_dve, by_act = (self.sem(c, n) for n in ("filled", "by_dve", "by_act"))
            stored, back = self.sem(c, "stored"), self.sem(c, "back")
            block = c.enter_context(nc.Block())
            w = self.w_qkv_b if causal else self.w_qkv
            bias = self.b_qkv_b if causal else self.b_qkv
            norms = 1 if causal else 2
            TJ = TILES // 4

            @block.tensor
            def _(pe):
                for j in range(TJ):
                    for t in range(4 * j, 4 * j + 4):
                        pe.wait_ge(s["normed"], (norms - 1) * TILES + t + 1)
                        last = nc.tensor.transpose(bank[j][:, (t % 4) * P:(t % 4 + 1) * P], xn[:, t, :], self.ident[:])
                    last.then_inc(filled, 1)
                for t in range(TILES):
                    if t % 4 == 0:
                        pe.wait_ge(by_act, t // 4 + 1)
                    if t >= 4:
                        pe.wait_ge(by_dve, t - 3)
                    nc.tensor.matmul(bank[4 + t % 4][:, 0:3 * D], xt[:, t, :], w[:], start=True,
                                     stop=True).then_inc(filled, 1)

            @block.scalar
            def _(act):
                for j in range(TJ):
                    act.wait_ge(filled, j + 1)
                    dst = xt[:, 4 * j:4 * j + 4, :].rearrange("p t r -> p (t r)")
                    if causal:
                        nc.scalar.activation(dst, bank[j][:], ACT.Identity).then_inc(by_act, 1)
                    else:
                        nc.scalar.activation(dst, bank[j][:], ACT.Identity, bias=self.ln_b[:],
                                             scale=self.ln_g[:]).then_inc(by_act, 1)

            @block.gpsimd
            def _(pool):
                for n in range(norms):
                    self.layernorm_pool(pool, s, n)

            @block.vector
            def _(dve):
                self.layernorm_dve(dve, self.x, xn, s, 0)
                if not causal:
                    dve.wait_ge(s["normed"], TILES)
                    self.layernorm_dve(dve, xn, xn, s, 1)
                for t in range(TILES):
                    dve.wait_ge(filled, TJ + t + 1)
                    src = bank[4 + t % 4][:, 0:3 * D]
                    if causal:
                        nc.vector.tensor_tensor(rows[:, t, :], src, bias[:], ALU.add).then_inc(by_dve, 1)
                    else:
                        b, tt = t // TPB, t % TPB
                        half = qkv[:, 4 * b:4 * b + 4].rearrange("p q (u t h) e -> p (q u) t h e", u=2, h=2)
                        for n in range(3):
                            cut = lambda v: v.rearrange("p (s u h e) -> p s u h e", s=3, h=2, e=HD)[:, n]
                            ins = nc.vector.tensor_tensor(half[:, :, tt, :, n * HD:(n + 1) * HD], cut(src),
                                                          cut(bias[:]), ALU.add)
                        ins.then_inc(by_dve, 1)

            @block.sync
            def _(sp):
                if causal:
                    per = TILES // QUADS
                    by_row = self.scratch_qkv.rearrange("(t p) f -> p t f", p=P)
                    by_pos = self.scratch_qkv.rearrange("r (c f) -> (r c) f", f=24) \
                                             .rearrange("(i n p) f -> p i n f", p=P, i=QUADS)
                    for i in range(QUADS):
                        sp.wait_ge(by_dve, per * (i + 1))
                        sp.dma_start(by_row[:, per * i:per * i + per, :], rows[:, per * i:per * i + per, :]) \
                          .then_inc(stored, 16)
                    for i in range(QUADS):
                        sp.wait_ge(stored, 16 * QUADS)
                        dst = qkv[:, i].rearrange("p (u t h) f -> p u h t f", u=2, h=2)
                        for g in range(4):
                            sp.dma_start(dst[:, g // 2, g % 2], by_pos[:, i, g * TPB:(g + 1) * TPB]).then_inc(back, 16)
                    sp.wait_ge(back, 16 * QUADS * 4)

    def attention(self, causal, qkv, y):
        nc = self.nc
        scale = 1.0 / (2.0 * D) ** 0.5 if causal else 1.0 / HD ** 0.5
        with ExitStack() as c:
            sb, sem = self.sb, self.sem
            q_stack = [sb(c, "q_stack", [P, 2, TPB, 2, STACK], BF16) for _ in range(2)]
            k_stack = [sb(c, "k_stack", [P, 2, TPB, 2, STACK], BF16) for _ in range(2)]
            v_aug = [sb(c, "v_aug", [P, 2, TPB, 2, 32]) for _ in range(2)]
            rest = sb(c, "rest", [P, 4 * TPB, HD])
            kt = [sb(c, "kt", [P, 2, SEQ], BF16) for _ in range(2)]
            qt_max = sb(c, "qt_max", [P, 2, SEQ], BF16)
            qt = [sb(c, "qt", [P, 2, SEQ], BF16) for _ in range(2)]
            mx = sb(c, "mx", [P, 2, TPB, 2])
            NP = 8
            probs = sb(c, "probs", [P, NP, BANK])
            ysum = sb(c, "ysum", [P, BANK])
            yrec = sb(c, "yrec", [P, 2, 4, 4])
            self.names += 1
            unit = [c.enter_context(nc.psum_tensor(f"unit{u}_{self.names}", [P, 2 * BANK], F32)) for u in range(2)]
            score = [c.enter_context(nc.psum_tensor(f"score{u}_{self.names}", [P, BANK], F32)) for u in range(3)]
            weighted = c.enter_context(nc.psum_tensor(f"weighted_{self.names}", [P, BANK], F32))

            blank, link, k_built, q_built, v_built = (sem(c, n) for n in ("blank", "link", "k_built", "q_built", "v_built"))
            unit_filled, unit_done = sem(c, "unit_filled"), sem(c, "unit_done")
            shift_link, shift_ready = sem(c, "shift_link"), sem(c, "shift_ready")
            scores_ready, probs_ready, probs_used = (sem(c, n) for n in ("scores_ready", "probs_ready", "probs_used"))
            sum_copied, norm_link = sem(c, "sum_copied"), sem(c, "norm_link")
            stored = sem(c, "stored")
            block = c.enter_context(nc.Block())

            SLOTS = [(qh, kb, max(0, kb * P - qh * BANK) if causal else 0) for qh in range(2) for kb in range(TPB)
                     if not causal or kb * P < (qh + 1) * BANK]
            NS = len(SLOTS)
            UNITS = 4 * NS
            HALF0 = sum(qh == 0 for qh, _, _ in SLOTS)
            diag = lambda qh, kb: causal and kb * P >= qh * BANK

            SPREAD = 0.94
            PREP = [("k", 0), ("q", 0), ("k", 1), ("q", 1)]
            PREP += [("max", 0, t, g) for t in range(TPB) for g in range(2)]
            PREP += [("max", 1, t, g) for t in range(2) for g in range(2)]
            PREP += [("shifted", 0)]
            PREP += [("max", 1, t, g) for t in range(2, TPB) for g in range(2)]
            PREP += [("shifted", 1)]
            NPREP = len(PREP)
            JOBS = NPREP + 2

            def columns(job):
                return {"max": 80 + ((job[2] + 1) * P if causal else SEQ) if job[0] == "max" else 0,
                        "y": 500}.get(job[0], 80 + SEQ // 2)

            def step_jobs(first, prep, last):
                by_place = [[] for _ in range(2 * NS + 1)]
                if prep:
                    jobs = PREP[:-1] + [("y", 0)] + PREP[-1:]
                    whole = sum(map(columns, jobs))
                    reach = sum(BANK - off for _, _, off in SLOTS)
                    ends, done = [], 0
                    for _, _, off in SLOTS:
                        for _ in range(2):
                            done += (BANK - off) / 2
                            ends.append(done / reach)
                    spent = 0
                    for job in jobs:
                        at = spent / whole * SPREAD
                        by_place[next(k for k, e in enumerate(ends) if e > at)].append(job)
                        spent += columns(job)
                else:
                    by_place[2 * (HALF0 + 2)].append(("y", 0))
                if not first:
                    by_place[4].insert(0, ("y", 1))
                if last:
                    by_place[2 * NS].append(("y", 1))
                return by_place

            def jobs_before(i):
                return NPREP if type(i) is int and i == 0 else JOBS * i + NPREP - 1

            def job_parity(i):
                return NPREP % 2 if type(i) is int and i == 0 else (NPREP - 1) % 2
            assert JOBS % 2 == 0

            def same_bank_before(u):
                if u >= 3:
                    return 3
                return next(UNITS - v for v in range(UNITS - 1, -1, -1) if v % 3 == u) + u

            def build(pool, i, par, links):
                n = [0]

                def chained(ins):
                    ins.then_inc(link, 1)
                    n[0] += 1
                    pool.wait_ge(link, links + n[0])

                if i >= 2:
                    pool.wait_ge(unit_filled, JOBS * i - 2 * JOBS + NPREP)
                for stack, off, his, mids, lo in ((k_stack[par], HD, (1, 4, 6), (2, 5), 3),
                                                  (q_stack[par], 0, (1, 2, 3), (4, 5), 6)):
                    src = qkv[:, i, :, off:off + HD]
                    part = lambda k: stack[:, :, :, :, 8 * k:8 * k + 8].rearrange("p u t h e -> p (u t h) e")
                    chained(nc.gpsimd.tensor_copy(part(his[0]), src))
                    for k in his[1:]:
                        nc.gpsimd.tensor_copy(part(k), part(his[0])).then_inc(link, 1)
                        n[0] += 1
                    chained(nc.gpsimd.tensor_tensor(rest[:], src, part(his[0]), ALU.subtract))
                    chained(nc.gpsimd.tensor_copy(part(mids[0]), rest[:]))
                    nc.gpsimd.tensor_copy(part(mids[1]), part(mids[0])).then_inc(link, 1)
                    n[0] += 1
                    chained(nc.gpsimd.tensor_tensor(rest[:], rest[:], part(mids[0]), ALU.subtract))
                    nc.gpsimd.tensor_copy(part(lo), rest[:]).then_inc(k_built if off else q_built, 1)
                    pool.wait_ge(k_built if off else q_built, i + 1)
                if i >= 2:
                    pool.wait_ge(probs_used, UNITS * i - UNITS)
                nc.gpsimd.tensor_copy(v_aug[par][:, :, :, :, 0:HD].rearrange("p u t h e -> p (u t h) e"),
                                      qkv[:, i, :, 2 * HD:3 * HD]) \
                  .then_inc(v_built, 1)
                return n[0]

            @block.gpsimd
            def _(pool):
                for b in range(2):
                    nc.gpsimd.memset(k_stack[b][:], 0.0).then_inc(blank, 1)
                    nc.gpsimd.memset(q_stack[b][:], 0.0).then_inc(blank, 1)
                    nc.gpsimd.memset(v_aug[b][:], 0.0).then_inc(blank, 1)
                pool.wait_ge(blank, 6)
                for b in range(2):
                    nc.gpsimd.memset(k_stack[b][:, :, :, :, 0:2], 1.0).then_inc(blank, 1)
                    nc.gpsimd.memset(v_aug[b][:, :, :, :, HD:HD + 1], 1.0).then_inc(blank, 1)
                pool.wait_ge(blank, 10)
                per = build(pool, 0, 0, 0)
                for i in range(1, QUADS):
                    build(pool, i, i % 2, i * per)

            def scores_of(pe, i, par, slot, first, heads):
                qh, kb, off = SLOTS[slot]
                for g in heads:
                    u = 4 * slot + g
                    back = same_bank_before(u)
                    if not (first and u < 3):
                        pe.wait_ge(probs_ready, i * UNITS + (u - back + 1))
                    rows = slice(64 * (g % 2), 64 * (g % 2) + STACK_USED)
                    out = score[u % 3]
                    ins = nc.tensor.matmul(out[:, off:BANK], kt[par][rows, g // 2, kb * P:kb * P + P],
                                           qt[par][rows, g // 2, qh * BANK + off:(qh + 1) * BANK],
                                           start=True, stop=not diag(qh, kb))
                    if diag(qh, kb):
                        ins = nc.tensor.matmul(out[:, off:off + P], self.identb[:], self.mask_kq[:],
                                               start=False, stop=True)
                    ins.then_inc(scores_ready, 1)

            def weigh(pe, i, par, slot, first):
                qh, kb, off = SLOTS[slot]
                if slot == 0:
                    pe.wait_ge(v_built, i + 1)
                    if not first:
                        pe.wait_ge(sum_copied, 2 * i)
                if slot == HALF0:
                    pe.wait_ge(sum_copied, 2 * i + 1)
                for g in range(4):
                    u = 4 * slot + g
                    pe.wait_ge(probs_ready, i * UNITS + u + 1)
                    nc.tensor.matmul(weighted[32 * g:32 * g + 32, off:BANK], v_aug[par][:, g // 2, kb, g % 2, :],
                                     probs[:, u % NP, off:BANK], start=kb == 0,
                                     stop=slot in (HALF0 - 1, NS - 1)).then_inc(probs_used, 1)

            def unit_job(pe, job, number, static_number, i_prep, par_prep, i):
                ubuf = unit[static_number % 2]
                if not (type(number) is int and number < 2):
                    pe.wait_ge(unit_done, number - 1)
                kind = job[0]
                if kind in ("k", "q", "shifted"):
                    pair = job[1]
                    if kind == "k":
                        pe.wait_ge(k_built, i_prep + 1)
                        src = k_stack[par_prep]
                    else:
                        src = q_stack[par_prep]
                        if kind == "q":
                            pe.wait_ge(q_built, i_prep + 1)
                        else:
                            pe.wait_ge(shift_ready, 2 * i_prep + pair + 1)
                    dst = ubuf[:].bitcast(BF16)
                    for t in range(TPB):
                        ins = nc.tensor.transpose(dst[:, t * P:(t + 1) * P], src[:, pair, t, :, :].rearrange("p h k -> p (h k)"),
                                                  self.identb[:])
                elif kind == "max":
                    _, pair, t, g = job
                    if t == 0 and g == 0:
                        pe.wait_ge(unit_done, number - max_since[pair])
                    rows = slice(64 * g, 64 * g + STACK_USED)
                    width = (t + 1) * P if causal else SEQ
                    for h in range(0, width, BANK):
                        end = min(h + BANK, width)
                        on_diag = causal and end == width
                        ins = nc.tensor.matmul(ubuf[:, h:end], qt_max[rows, pair, t * P:t * P + P],
                                               kt[par_prep][rows, pair, h:end], start=True, stop=not on_diag)
                        if on_diag:
                            ins = nc.tensor.matmul(ubuf[:, width - P:width], self.identb[:], self.mask_qk[:],
                                                   start=False, stop=True)
                else:
                    half = job[1]
                    pe.wait_ge(sum_copied, 2 * i + half + 1)
                    for t in range(4):
                        ins = nc.tensor.transpose(ubuf[:, t * P:(t + 1) * P], ysum[:, t * P:(t + 1) * P], self.ident[:])
                ins.then_inc(unit_filled, 1)

            max_since = {p: PREP.index(("max", p, 0, 0)) - PREP.index(("q", p)) - 1 for p in range(2)}

            def walk(i, first, prep, last):
                n = 0
                for place, jobs in enumerate(step_jobs(first, prep, last)):
                    for job in jobs:
                        quad = i + 1
                        if job[0] == "y":
                            quad = i - 1 if job[1] == 1 and place < 2 * NS else i
                        yield place, job, jobs_before(i) + n, job_parity(i) + n, quad
                        n += 1

            def pe_step(pe, i, par, first=False, prep=True, last=False):
                jobs = list(walk(i, first, prep, last))

                def jobs_at(place):
                    for at, job, number, static, quad in jobs:
                        if at == place:
                            unit_job(pe, job, number, static, quad, 1 - par, quad)

                pe.wait_ge(unit_done, jobs_before(i))
                for slot in range(NS):
                    scores_of(pe, i, par, slot, first, (0, 1))
                    jobs_at(2 * slot)
                    scores_of(pe, i, par, slot, first, (2, 3))
                    if slot:
                        weigh(pe, i, par, slot - 1, first)
                    elif not first:
                        weigh(pe, i - 1, 1 - par, NS - 1, False)
                    jobs_at(2 * slot + 1)
                if last:
                    weigh(pe, i, par, NS - 1, first)
                    jobs_at(2 * NS)

            def drive(engine, step):
                step(engine, 0, 0, first=True)
                with engine.Fori(1, QUADS - 1, 2) as i:
                    step(engine, i, 1)
                    step(engine, i + 1, 0)
                step(engine, QUADS - 1, 1, prep=False, last=True)

            @block.tensor
            def _(pe):
                pe.wait_ge(blank, 10)
                for n, job in enumerate(PREP):
                    unit_job(pe, job, n, n, 0, 0, 0)
                drive(pe, pe_step)

            flat = [job for jobs in step_jobs(False, True, False) for job in jobs]
            Y1_AT, Y0_AT = flat.index(("y", 1)), flat.index(("y", 0))

            def copy_sums(act, i, half, first=False, alone=False):
                act.wait_ge(probs_used, i * UNITS + (UNITS if half else 4 * HALF0))
                if half:
                    act.wait_ge(unit_filled, jobs_before(i) + 2 if alone else JOBS * i + NPREP + Y0_AT)
                elif not first:
                    act.wait_ge(unit_filled, jobs_before(i) + (0 if alone else Y1_AT) + 1)
                nc.scalar.activation(ysum[:], weighted[:], ACT.Copy).then_inc(sum_copied, 1)

            def act_step(act, i, par, first=False, prep=True, last=False):
                for slot in range(NS):
                    qh, kb, off = SLOTS[slot]
                    for g in range(4):
                        u = 4 * slot + g
                        act.wait_ge(scores_ready, i * UNITS + u + 1)
                        if not (first and u < NP):
                            act.wait_ge(probs_used, i * UNITS + (u - NP + 1))
                        nc.scalar.activation(probs[:, u % NP, off:BANK], score[u % 3][:, off:BANK], ACT.Exp,
                                             scale=scale).then_inc(probs_ready, 1)
                        if slot == 1 and g == 1 and not first:
                            copy_sums(act, i - 1, 1)
                        if slot == HALF0 + 1 and g == 1:
                            copy_sums(act, i, 0, first, not prep)
                if last:
                    copy_sums(act, i, 1, alone=True)

            @block.scalar
            def _(act):
                drive(act, act_step)

            def dve_job(dve, job, number, static_number, par_prep, quad, norms):
                ubuf = unit[static_number % 2]
                dve.wait_ge(unit_filled, number + 1)
                kind = job[0]
                if kind in ("k", "q", "shifted"):
                    pair = job[1]
                    dst = {"k": kt[par_prep], "q": qt_max, "shifted": qt[par_prep]}[kind]
                    nc.vector.tensor_copy(dst[:, pair, :], ubuf[:].bitcast(BF16)[:, 0:SEQ]).then_inc(unit_done, 1)
                elif kind == "max":
                    _, pair, t, g = job
                    width = (t + 1) * P if causal else SEQ
                    nc.vector.reduce_max(mx[:, pair, t, g:g + 1], ubuf[:, 0:width], AXX).then_inc(unit_done, 1)
                    if t == TPB - 1 and g == 1:
                        dve.wait_ge(unit_done, number + 1)
                        m = mx[:, pair].rearrange("p t h -> p (t h)")
                        hi = q_stack[par_prep][:, pair, :, :, 0].rearrange("p t h -> p (t h)")
                        lo = q_stack[par_prep][:, pair, :, :, 1].rearrange("p t h -> p (t h)")
                        nc.vector.tensor_scalar(hi, m, -1.0, None, ALU.mult).then_inc(shift_link, 1)
                        dve.wait_ge(shift_link, 2 * quad + pair + 1)
                        nc.vector.scalar_tensor_tensor(out=lo, in0=m, scalar=-1.0, in1=hi, op0=ALU.mult,
                                                       op1=ALU.subtract).then_inc(shift_ready, 1)
                else:
                    half = job[1]
                    sums = ubuf[:, 0:BANK].rearrange("p (t g e) -> p t g e", t=4, g=4)
                    nc.vector.reciprocal(yrec[:, half], sums[:, :, :, HD]).then_inc(norm_link, 1)
                    dve.wait_ge(norm_link, 2 * quad + half + 1)
                    dst = y[:, quad, 4 * half:4 * half + 4, :].rearrange("p t (g e) -> p t g e", g=4)
                    rec = yrec[:, half].unsqueeze(3).broadcast_to([P, 4, 4, HD])
                    nc.vector.tensor_tensor(dst, sums[:, :, :, 0:HD], rec, ALU.mult).then_inc(unit_done, 1)

            def dve_step(dve, i, par, first=False, prep=True, last=False):
                for s, job, number, static, quad in walk(i, first, prep, last):
                    dve_job(dve, job, number, static, 1 - par, quad, None)

            @block.vector
            def _(dve):
                for n, job in enumerate(PREP):
                    dve_job(dve, job, n, n, 0, 0, None)
                drive(dve, dve_step)

            total = JOBS * QUADS
            @block.sync
            def _(sp):
                if causal:
                    sp.wait_ge(unit_done, total)
                    dst = self.scratch_y.rearrange("(n p e) -> p n e", p=P, e=HD)
                    for i in range(QUADS):
                        for t in range(TPB):
                            sp.dma_start(dst[:, i * 32:(i + 1) * 32, :].rearrange("p (g t) e -> p t g e", g=4)[:, t],
                                         y[:, i, t, :].rearrange("p (g e) -> p g e", g=4)).then_inc(stored, 16)
                    sp.wait_ge(stored, 16 * QUADS * TPB)

    def residual(self, causal, y):
        nc = self.nc
        with ExitStack() as c:
            rows = self.sb(c, "yrows", [P, TILES, D])
            back, added = self.sem(c, "back"), self.sem(c, "added")
            block = c.enter_context(nc.Block())

            @block.sync
            def _(sp):
                if causal:
                    sp.dma_start(rows[:], self.scratch_y.rearrange("(t p d) -> p t d", p=P, d=D)).then_inc(back, 16)

            @block.vector
            def _(dve):
                if causal:
                    dve.wait_ge(back, 16)
                    nc.vector.tensor_tensor(self.x[:], self.x[:], rows[:], ALU.add).then_inc(added, 1)
                else:
                    for b in range(BATCH):
                        xv = self.x[:, b * TPB:(b + 1) * TPB, :].rearrange("p t (q e) -> p q t e", q=4)
                        nc.vector.tensor_tensor(xv, xv, y[:, 4 * b:4 * b + 4], ALU.add).then_inc(added, 1)

    def mixture(self, final):
        nc = self.nc
        NT = 16
        with ExitStack() as c:
            sb, sem = self.sb, self.sem
            tok = sb(c, "tok", [P, 4 * NT, D1])
            fa = sb(c, "fa", [P, 8192])
            fb = sb(c, "fb", [P, 8192])
            diag = sb(c, "diag", [P, 2, 2048])
            hid = sb(c, "hid", [P, P, F1])
            xn = hid[:, 0:32, :].rearrange("p (t a) d -> p t (a d)", t=TILES)
            xt = hid[:, 32:64, :].rearrange("p (t a) r -> p t (a r)", t=TILES)
            yt = tok[:].rearrange("p n i -> p (n i)").rearrange("p (d n o) -> p d n o", d=2, o=D1)
            logit_t = sb(c, "logit_t", [P, P])
            logit = sb(c, "logit", [P, 2, EXPERTS])
            top = sb(c, "top", [P, 2, 8])
            index = sb(c, "index", [P, 2, 8], U32)
            indexf = sb(c, "indexf", [P, 2, 2])
            gap = sb(c, "gap", [P, 4, 2])
            one_w = sb(c, "one_w", [P, 2, 2, EXPERTS])
            one_b = sb(c, "one_b", [P, 2, 2, 2 * EXPERTS], BF16)
            pick = sb(c, "pick", [P, 2, 512], BF16)
            pick_w = sb(c, "pick_w", [EXPERTS, 512])
            weight = sb(c, "weight", [P, 256])
            s = self.layernorm_state(c)
            bank = self.banks(c)
            filled, by_dve, by_act = sem(c, "filled"), sem(c, "by_dve"), sem(c, "by_act")
            top_link, exp_ready, gelu_done, zeroed = (sem(c, n) for n in ("top_link", "exp_ready", "gelu_done", "zeroed"))
            stored = sem(c, "stored")
            block = c.enter_context(nc.Block())

            JOBS = [("xt", j) for j in range(4)] + [("tok", j) for j in range(4)]
            JOBS += [("route", 0), ("pick", 0, 0), ("pick", 0, 1), ("weigh", 0)]
            JOBS += [("fetch_up", w, j) for j in range(16) for w in range(2)]
            JOBS += [("first_up", 0)]
            for j in range(16):
                JOBS += [("first_up", j + 1)] * (j < 15) + [("second_up", j)]
            JOBS += [("logits", 0), ("route", 1), ("pick", 1, 0), ("pick", 1, 1), ("weigh", 1)]
            for h in range(2):
                JOBS += [("fetch_down", h, w, j) for j in range(8) for w in range(2)]
                for j in range(8):
                    JOBS += [("first_down", h, j)]
                    if j == 4:
                        JOBS += [("second_down", h, 0)]
                JOBS += [("second_down", h, 1)]
            JOBS += [("back", w) for w in range(4)]
            number = {job: n for n, job in enumerate(JOBS)}

            def on_act_(job):
                kind = job[0]
                if kind in ("xt", "tok"):
                    return job[1] % 2 == 1
                if kind == "fetch_up":
                    return job[1] == 1
                if kind == "fetch_down":
                    return job[2] == 0
                return kind in ("first_up", "first_down") and job[-1] % 2 == 1
            on_act = [on_act_(job) for job in JOBS]

            def emptied(eng, job):
                n = number[job]
                if on_act[n]:
                    eng.wait_ge(by_act, sum(on_act[:n + 1]))
                else:
                    eng.wait_ge(by_dve, n + 1 - sum(on_act[:n + 1]))

            def all_emptied(eng, jobs):
                for who in (False, True):
                    of = [j for j in jobs if on_act[number[j]] == who]
                    if of:
                        emptied(eng, max(of, key=number.get))

            def bank_free(pe, job):
                n = number[job]
                if n >= 8:
                    emptied(pe, JOBS[n - 8])
                return bank[n % 8]

            def fetch(b, rows, cols, table, at, width, picked):
                nc.tensor.matmul(b[rows, cols], self.tab_hm[table][:, at:at + width], picked, start=True, stop=False)
                return nc.tensor.matmul(b[rows, cols], self.tab_lo[table][:, at:at + width], picked,
                                        start=False, stop=True)

            def up_tokens(j):
                return [(half, 2 * j + e) for half in range(2) for e in range(2)]

            def second_down_part(b, h, j):
                for x in range(4):
                    m2 = 4 * j + x
                    for half in range(2):
                        w = 2 * half + m2 % 2
                        out = b[32 * w:32 * w + 32, :].rearrange("p (d n o) -> p d n o", d=2, n=8)[:, :, (m2 // 2) % 8, :]
                        for k in range(2):
                            pair = (half * 32 + m2) * 2 + k
                            ins = nc.tensor.matmul(out, fb[:, pair * D1:(pair + 1) * D1],
                                                   diag[:, j % 2, (x * 4 + half * 2 + k) * 64:(x * 4 + half * 2 + k + 1) * 64],
                                                   start=k == 0, stop=k == 1)
                return ins

            @block.tensor
            def _(pe):
                for n, job in enumerate(JOBS):
                    kind = job[0]
                    b = bank_free(pe, job)
                    if kind == "xt":
                        for t in range(4 * job[1], 4 * job[1] + 4):
                            pe.wait_ge(s["normed"], t + 1)
                            ins = nc.tensor.transpose(b[:, (t % 4) * P:(t % 4 + 1) * P], xn[:, t, :], self.ident[:])
                    elif kind == "tok":
                        for c4 in range(4):
                            for g in range(4):
                                ins = nc.tensor.matmul(b[32 * g:32 * g + 32, c4 * P:(c4 + 1) * P],
                                                       xn[:, 4 * job[1] + g, 32 * c4:32 * c4 + 32], self.ident[:],
                                                       start=True, stop=True)
                    elif job == ("route", 0):
                        all_emptied(pe, [("xt", j) for j in range(4)])
                        for half in range(2):
                            v = xt[:, 8 * half:8 * half + 8, :].rearrange("c t (n r) -> c (t n) r", r=TOKROWS)
                            for r in range(TOKROWS):
                                ins = nc.tensor.matmul(b[:, half * EXPERTS:(half + 1) * EXPERTS], v[:, :, r],
                                                       self.router_up[:, r, :], start=r == 0, stop=r == TOKROWS - 1)
                    elif kind == "logits":
                        pe.wait_ge(gelu_done, 16)
                        for p in range(F1):
                            for half in range(2):
                                rows = slice(64 * half, 64 * half + 64)
                                ins = nc.tensor.matmul(b[rows, 0:P], self.router_dn[rows, p, :], hid[rows, :, p],
                                                       start=p == 0, stop=p == F1 - 1)
                    elif job == ("route", 1):
                        emptied(pe, ("logits", 0))
                        ins = nc.tensor.transpose(b[:, 0:P], logit_t[:], self.ident[:])
                    elif kind == "pick":
                        _, layer, half = job
                        pe.wait_ge(top_link, ROUTED * (layer + 1))
                        for k in range(2):
                            nc.tensor.transpose(b[:].bitcast(BF16)[:, k * P:(k + 1) * P], one_b[:, half, k, :],
                                                self.identb[:])
                        for k in range(2):
                            ins = nc.tensor.transpose(b[0:EXPERTS, (k + 1) * P:(k + 2) * P], one_w[:, half, k, :],
                                                      self.ident[:])
                    elif kind == "weigh":
                        all_emptied(pe, [("pick", job[1], half) for half in range(2)])
                        if job[1] == 0:
                            for g in range(4):
                                ins = nc.tensor.matmul(b[32 * g:32 * g + 32, 0:P], self.ones[:, 0:32],
                                                       pick_w[:, g * P:(g + 1) * P], start=True, stop=True)
                        else:
                            for h in range(2):
                                for d in range(2):
                                    ins = nc.tensor.matmul(b[64 * d:64 * d + 64, h * P:(h + 1) * P], self.ones[:],
                                                           pick_w[:, (2 * h + d) * P:(2 * h + d + 1) * P],
                                                           start=True, stop=True)
                    elif kind == "fetch_up":
                        _, w, j = job
                        for o in range(4):
                            for g in range(4):
                                ins = fetch(b, slice(32 * g, 32 * g + 32), slice(o * P, (o + 1) * P), "B_up" if w else "A_up",
                                            (4 * j + o) * D1, D1, pick[:, 0, g * P:(g + 1) * P])
                    elif kind == "first_up":
                        j = job[1]
                        if j == 0:
                            all_emptied(pe, [("tok", q) for q in range(4)])
                            all_emptied(pe, [("fetch_up", w, k) for w in range(2) for k in range(16)])
                        for t, (half, e) in enumerate(up_tokens(j)):
                            n_tok = 32 * half + e
                            for g in range(4):
                                rows = slice(32 * g, 32 * g + 32)
                                ins = nc.tensor.matmul(b[rows, t * P:(t + 1) * P], tok[rows, n_tok, :],
                                                       fb[rows, n_tok * P:(n_tok + 1) * P], start=True, stop=True)
                    elif kind == "second_up":
                        j = job[1]
                        emptied(pe, ("first_up", j))
                        for e in range(2):
                            for k in range(2):
                                for half in range(2):
                                    n_tok, t = 32 * half + 2 * j + e, 2 * half + e
                                    ins = nc.tensor.matmul(b[64 * half:64 * half + 64, e * 256:(e + 1) * 256],
                                                           fa[:, n_tok * P + k * F1:n_tok * P + (k + 1) * F1],
                                                           diag[:, j % 2, (2 * t + k) * 256:(2 * t + k + 1) * 256],
                                                           start=k == 0, stop=k == 1)
                    elif kind == "fetch_down":
                        _, h, w, j = job
                        for o in range(4):
                            for half in range(2):
                                picked = pick[:, 1, (2 * h + half) * P:(2 * h + half + 1) * P] if w else \
                                    pick[:, 0, half * 256 + h * P:half * 256 + (h + 1) * P]
                                ins = fetch(b, slice(64 * half, 64 * half + 64), slice(o * P, (o + 1) * P),
                                            "B_down" if w else "A_down", (4 * j + o) * F1, F1, picked)
                    elif kind == "first_down":
                        _, h, j = job
                        if j == 0:
                            all_emptied(pe, [("fetch_down", h, w, k) for w in range(2) for k in range(8)])
                        for x in range(4):
                            for d in range(2):
                                m = 8 * j + 2 * x + d
                                ins = nc.tensor.matmul(b[64 * d:64 * d + 64, x * P:(x + 1) * P], hid[:, 64 * h + m, :],
                                                       fa[:, m * P:(m + 1) * P], start=True, stop=True)
                        ins.then_inc(filled, 1)
                        if j:
                            into = ("second_down", h, (j - 1) // 4)
                            if (j - 1) % 4 == 0:
                                bank_free(pe, into)
                            emptied(pe, ("first_down", h, j - 1))
                            ins = second_down_part(bank[number[into] % 8], h, j - 1)
                            if (j - 1) % 4 == 3:
                                ins.then_inc(filled, 1)
                        continue
                    elif kind == "second_down":
                        _, h, part = job
                        if part == 0:
                            continue
                        emptied(pe, ("first_down", h, 7))
                        ins = second_down_part(b, h, 7)
                    elif kind == "back":
                        w = job[1]
                        rows = slice(32 * w, 32 * w + 32)
                        if w == 0:
                            emptied(pe, ("second_down", 1, 1))
                        for q2 in range(2):
                            for d in range(2):
                                v = yt[:, d, q2 * NT:(q2 + 1) * NT, :].rearrange("p n (r c) -> p (n r) c", c=4)
                                for c4 in range(4):
                                    at = (2 * q2 + d) * P + c4 * D1
                                    ins = nc.tensor.transpose(b[:, at:at + D1], v[rows, :, c4], self.ident[rows, rows])
                    ins.then_inc(filled, 1)

            def route(dve, b, layer, done):
                count = [ROUTED * layer]

                def step(*many):
                    for ins in many:
                        count[0] += 1
                        ins.then_inc(top_link, 1)
                    dve.wait_ge(top_link, count[0])

                nc.vector.tensor_copy(logit[:].rearrange("p h e -> p (h e)"), b[:, 0:2 * EXPERTS]).then_inc(by_dve, 1)
                dve.wait_ge(by_dve, done)
                step(*[nc.vector.max(top[:, h, :], logit[:, h, :]) for h in range(2)])
                step(*[nc.vector.max_index(index[:, h, :], top[:, h, :], logit[:, h, :]) for h in range(2)])
                step(nc.vector.tensor_copy(indexf[:], index[:, :, 0:2]),
                     nc.vector.tensor_tensor(gap[:, 0, :], top[:, :, 1], top[:, :, 0], ALU.subtract))
                dve.wait_ge(exp_ready, layer + 1)
                step(nc.vector.tensor_scalar(gap[:, 2, :], gap[:, 1, :], 1.0, None, ALU.add))
                step(nc.vector.reciprocal(gap[:, 2, :], gap[:, 2, :]))
                step(nc.vector.tensor_tensor(gap[:, 3, :], gap[:, 1, :], gap[:, 2, :], ALU.mult))
                for h in range(2):
                    for k in range(2):
                        nc.vector.tensor_scalar(one_w[:, h, k, :], self.iota_e[:, 0:EXPERTS], indexf[:, h, k:k + 1],
                                                gap[:, 2 + k, h:h + 1], ALU.is_equal, ALU.mult).then_inc(top_link, 1)
                        nc.vector.tensor_scalar(one_b[:, h, k, :], self.iota_e[:], indexf[:, h, k:k + 1],
                                                None, ALU.is_equal).then_inc(top_link, 1)
                        count[0] += 2
                assert count[0] == ROUTED * (layer + 1)

            def pick_up(view, half, k):
                return view.rearrange("e (g q t k) -> e q g t k", g=4, q=4, k=2)[:, 2 * half:2 * half + 2, :, :, k]

            def pick_plain(view, half, k):
                return view.rearrange("e (c m k) -> e c m k", c=2, k=2)[:, half, :, k]

            def pick_by_parity(view, half, k):
                return view.rearrange("e (h d c m k) -> e c h m d k", h=2, d=2, c=2, k=2)[:, half, :, :, :, k]

            def move(copy, job, b):
                kind = job[0]
                if kind == "xt":
                    return copy(xt[:, 4 * job[1]:4 * job[1] + 4, :].rearrange("p t r -> p (t r)"), b[:])
                if kind == "tok":
                    return copy(tok[:, NT * job[1]:NT * job[1] + NT, :].rearrange("p t (r c) -> p c (t r)", c=4),
                                b[:].rearrange("p (c r) -> p c r", c=4))
                if kind == "fetch_up":
                    return copy(fb[:].rearrange("p (n o) -> p o n", o=F1)[:, 4 * job[2]:4 * job[2] + 4, :],
                                b[:].rearrange("p (o n) -> p o n", o=4))
                if kind == "fetch_down":
                    for half in range(2):
                        rows = slice(64 * half, 64 * half + 64)
                        dst = fa[rows, :].rearrange("p (m c k o) -> p c o m k", c=2, k=2, o=D1)[:, half, 4 * job[3]:4 * job[3] + 4]
                        ins = copy(dst, b[rows, :].rearrange("p (o m k) -> p o m k", o=4, k=2))
                    return ins
                if kind == "first_up":
                    for g in range(4):
                        rows = slice(32 * g, 32 * g + 32)
                        dst = diag[rows, job[1] % 2, :].rearrange("p (t g q) -> p g t q", g=4, q=F1)[:, g]
                        ins = copy(dst, b[rows, :].rearrange("p (t q) -> p t q", q=F1))
                    return ins
                for d in range(2):
                    rows = slice(64 * d, 64 * d + 64)
                    dst = diag[rows, job[2] % 2, 0:1024].rearrange("p (t d q) -> p d t q", d=2, q=D1)[:, d]
                    ins = copy(dst, b[rows, :].rearrange("p (t q) -> p t q", q=D1))
                return ins

            def ready_to_move(eng, job):
                if job[0] == "first_up" and job[1] < 2:
                    eng.wait_ge(zeroed, 1)
                if job[0] == "fetch_down" and job[2] == 0 and job[3] == 0 and job[1] == 0:
                    eng.wait_ge(zeroed, 4)
                if job[0] == "first_down" and job[2] < 2 and job[1] == 0:
                    eng.wait_ge(zeroed, 4)

            @block.vector
            def _(dve):
                self.layernorm_dve(dve, self.x, xn, s, 0)
                done = 0
                for n, job in enumerate(JOBS):
                    if on_act[n]:
                        continue
                    done += 1
                    b = bank[n % 8]
                    kind = job[0]
                    dve.wait_ge(filled, n + 1)
                    ready_to_move(dve, job)
                    if kind == "route":
                        route(dve, b, job[1], done)
                        continue
                    if kind == "logits":
                        ins = nc.vector.tensor_copy(logit_t[:], b[:, 0:P])
                    elif kind == "pick":
                        _, layer, half = job
                        plain, weighted = b[:].bitcast(BF16), b[0:EXPERTS, P:3 * P]
                        for k in range(2):
                            src, src_w = plain[:, k * P:(k + 1) * P], weighted[:, k * P:(k + 1) * P]
                            if layer == 0:
                                cut = lambda v: v.rearrange("e (q g t) -> e q g t", q=2, g=4)
                                nc.vector.tensor_copy(pick_up(pick[:, 0, :], half, k), cut(src))
                                ins = nc.vector.tensor_copy(pick_up(pick_w[:], half, k), cut(src_w))
                            else:
                                cut = lambda v: v.rearrange("e (h m d) -> e h m d", h=2, d=2)
                                nc.vector.tensor_copy(pick_plain(pick[:, 0, :], half, k), src)
                                nc.vector.tensor_copy(pick_by_parity(pick[:, 1, :], half, k), cut(src))
                                ins = nc.vector.tensor_copy(pick_by_parity(pick_w[:], half, k), cut(src_w))
                    elif kind == "weigh":
                        width = P if job[1] == 0 else 2 * P
                        ins = nc.vector.tensor_copy(weight[:, 0:width], b[:, 0:width])
                    elif kind == "fetch_up":
                        j = job[2]
                        if j == 0:
                            emptied(dve, ("weigh", 0))
                        ins = nc.vector.tensor_tensor(fa[:].rearrange("p (n o) -> p o n", o=F1)[:, 4 * j:4 * j + 4, :],
                                                      b[:].rearrange("p (o n) -> p o n", o=4),
                                                      weight[:, 0:P].unsqueeze(1).broadcast_to([P, 4, P]), ALU.mult)
                    elif kind == "fetch_down":
                        _, h, _, j = job
                        if j == 0:
                            emptied(dve, ("weigh", 1))
                        ins = nc.vector.tensor_tensor(fb[:, 0:4096].rearrange("p (n o) -> p o n", o=D1)[:, 4 * j:4 * j + 4, :],
                                                      b[:].rearrange("p (o n) -> p o n", o=4),
                                                      weight[:, h * P:(h + 1) * P].unsqueeze(1).broadcast_to([P, 4, P]),
                                                      ALU.mult)
                    elif kind == "second_up":
                        bias = self.bias_up[:].unsqueeze(1).broadcast_to([P, 8, F1])
                        ins = nc.vector.scalar_tensor_tensor(out=hid[:, 8 * job[1]:8 * job[1] + 8, :],
                                                             in0=b[:].rearrange("p (t o) -> p t o", t=8),
                                                             scalar=self.scale_up[:], in1=bias, op0=ALU.mult, op1=ALU.add)
                    elif kind == "second_down":
                        at = 16 * job[1] + 8 * job[2]
                        for d in range(2):
                            bias = self.bias_dn[:].unsqueeze(1).broadcast_to([P, 8, D1])
                            ins = nc.vector.scalar_tensor_tensor(out=yt[:, d, at:at + 8, :],
                                                                 in0=b[:, d * 256:(d + 1) * 256].rearrange("p (n o) -> p n o", n=8),
                                                                 scalar=self.scale_dn[:], in1=bias, op0=ALU.mult,
                                                                 op1=ALU.add)
                    elif kind == "back":
                        half, gh = job[1] // 2, job[1] % 2
                        xv = self.x[:].rearrange("p (c q g d) e -> p c g q d e", c=2, q=2, g=2)[:, half, gh]
                        ins = nc.vector.tensor_tensor(xv, b[:].rearrange("p (q d e) -> p q d e", q=2, d=2), xv, ALU.add)
                    else:
                        ins = move(nc.vector.tensor_copy, job, b)
                    ins.then_inc(by_dve, 1)

            @block.scalar
            def _(act):
                copy = lambda dst, src: nc.scalar.activation(dst, src, ACT.Copy)
                for n, job in enumerate(JOBS):
                    b = bank[n % 8]
                    if on_act[n]:
                        act.wait_ge(filled, n + 1)
                        ready_to_move(act, job)
                        move(copy, job, b).then_inc(by_act, 1)
                    elif job[0] == "route":
                        act.wait_ge(top_link, ROUTED * job[1] + 6)
                        nc.scalar.activation(gap[:, 1, :], gap[:, 0, :], ACT.Exp).then_inc(exp_ready, 1)
                    elif job[0] == "second_up":
                        emptied(act, job)
                        v = hid[:, 8 * job[1]:8 * job[1] + 8, :]
                        nc.scalar.activation(v, v, ACT.Gelu).then_inc(gelu_done, 1)

            @block.gpsimd
            def _(pool):
                nc.gpsimd.memset(diag[:], 0.0).then_inc(zeroed, 1)
                self.layernorm_pool(pool, s, 0)
                pool.wait_ge(filled, number[("second_up", 15)] + 1)
                nc.gpsimd.memset(diag[:, :, 0:1024], 0.0).then_inc(zeroed, 1)
                for half in range(2):
                    pool.wait_ge(zeroed, 2 + half)
                    rows = slice(64 * half, 64 * half + 64)
                    v = fa[rows, :].rearrange("p (m c q) -> p c m q", c=2, q=2 * D1)[:, 1 - half]
                    nc.gpsimd.memset(v, 0.0).then_inc(zeroed, 1)

            @block.sync
            def _(sp):
                if final:
                    emptied(sp, ("back", 3))
                    sp.dma_start(self.out.rearrange("b (t p) d -> p (b t) d", p=P), self.x[:]).then_inc(stored, 16)
                    sp.wait_ge(stored, 16)

    def build(self):
        nc = self.nc
        self.scratch_qkv = nc.dram_tensor("scratch_qkv", [BATCH * SEQ, 3 * D], F32, kind="Internal").ap()
        self.scratch_y = nc.dram_tensor("scratch_y", [BATCH * SEQ * D], F32, kind="Internal").ap()
        with ExitStack() as ctx:
            self.setup(ctx)
            for causal in (False, True):
                with ExitStack() as c:
                    y = self.sb(c, "y", [P, QUADS, TPB, 32])
                    with ExitStack() as c2:
                        qkv = self.sb(c2, "qkv", [P, QUADS, 4 * TPB, 24])
                        self.project(causal, qkv)
                        self.attention(causal, qkv, y)
                    self.residual(causal, y)
                self.mixture(final=causal)


_INS = ["L0_attn_a_x", "L0_attn_a_ln_g", "L0_attn_a_ln_b", "L0_attn_a_Wq", "L0_attn_a_bq", "L0_attn_a_Wk",
        "L0_attn_a_bk", "L0_attn_a_Wv", "L0_attn_a_bv", "L0_attn_b_qkv_kernel", "L0_attn_b_qkv_bias",
        "L0_ffn_W_up", "L0_ffn_A_up", "L0_ffn_B_up", "L0_ffn_scale_up", "L0_ffn_bias_up", "L0_ffn_W_down",
        "L0_ffn_A_down", "L0_ffn_B_down", "L0_ffn_scale_down", "L0_ffn_bias_down"]


def kernel(**inputs):
    import numpy as _np
    import concourse.bacc as _bacc
    from concourse import mybir as _mybir
    from concourse.bass_utils import run_bass_kernel_spmd as _run

    nc = _bacc.Bacc("TRN2", target_bir_lowering=False, num_devices=1)
    arrays, aps = {}, {}
    for name in _INS:
        a = _np.ascontiguousarray(inputs[name])
        arrays[f"in_{name}"] = a
        aps[name] = nc.dram_tensor(f"in_{name}", a.shape, _mybir.dt.from_np(a.dtype), kind="ExternalInput").ap()
    out = nc.dram_tensor("out_0", (BATCH, SEQ, D), F32, kind="ExternalOutput").ap()
    Kernel(nc, aps, out).build()
    r = _run(nc, [arrays], core_ids=[0])
    return r.results[0]["out_0"]
```

```python
from contextlib import ExitStack

import concourse.bass as bass
from concourse import mybir

F32 = mybir.dt.float32
BF16 = mybir.dt.bfloat16
U32 = mybir.dt.uint32
ALU = mybir.AluOpType
ACT = mybir.ActivationFunctionType
AXX = mybir.AxisListType.X

P = 128
BATCH, SEQ, D = 2, 1024, 128
HEADS, HD = 16, 8
TILES = BATCH * SEQ // P
TPB = SEQ // P
QUADS = BATCH * HEADS // 4
EXPERTS = 64
D1, F1 = 32, 64
TOKROWS = D1 * D1 // D
EPS = 1e-5
MASKED = -1e30
TABLES = ("A_up", "B_up", "A_down", "B_down")
BANK = 512
STACK = 64
ROUTED = 17
CHUNKS, CH = 4, TILES // 4
CONSTANTS, BLANKS = 11, 10
STACK_USED = 56


class Kernel:
    def __init__(self, nc, a, out):
        self.nc, self.a, self.out = nc, a, out
        self.names = 0

    def sem(self, ctx, name):
        self.names += 1
        return ctx.enter_context(self.nc.semaphore(f"{name}_{self.names}"))

    def sb(self, ctx, name, shape, dt=F32):
        self.names += 1
        return ctx.enter_context(self.nc.sbuf_tensor(f"{name}_{self.names}", shape, dt))

    def banks(self, ctx, n=8):
        self.names += 1
        return [ctx.enter_context(self.nc.psum_tensor(f"bank{i}_{self.names}", [P, BANK], F32)) for i in range(n)]

    def setup(self, ctx):
        nc, a = self.nc, self.a
        sb = self.sb
        self.x = sb(ctx, "x", [P, TILES, D])
        self.ident = sb(ctx, "ident", [P, P])
        self.identb = sb(ctx, "identb", [P, P], BF16)
        self.mask_qk = sb(ctx, "mask_qk", [P, P], BF16)
        self.mask_kq = sb(ctx, "mask_kq", [P, P], BF16)
        self.half_neg = sb(ctx, "half_neg", [P, TILES])
        self.iota_e = sb(ctx, "iota_e", [P, 2 * EXPERTS])
        self.ones = sb(ctx, "ones", [EXPERTS, 64])
        self.w_qkv = sb(ctx, "w_qkv", [P, 3 * D])
        self.w_qkv_b = sb(ctx, "w_qkv_b", [P, 3 * D])
        self.b_qkv = sb(ctx, "b_qkv", [P, 3 * D])
        self.b_qkv_b = sb(ctx, "b_qkv_b", [P, 3 * D])
        self.ln_g = sb(ctx, "ln_g", [P, 1])
        self.ln_b = sb(ctx, "ln_b", [P, 1])
        self.router_up = sb(ctx, "router_up", [P, TOKROWS, EXPERTS])
        self.router_dn = sb(ctx, "router_dn", [P, F1, EXPERTS])
        self.tab_hm = {k: sb(ctx, k + "_hm", [P, F1 * D1], BF16) for k in TABLES}
        self.tab_lo = {k: sb(ctx, k + "_lo", [P, F1 * D1], BF16) for k in TABLES}
        self.bias_up = sb(ctx, "bias_up", [P, F1])
        self.bias_dn = sb(ctx, "bias_dn", [P, D1])
        self.scale_up = sb(ctx, "scale_up", [P, 1])
        self.scale_dn = sb(ctx, "scale_dn", [P, 1])
        self.made = self.sem(ctx, "made")
        self.later_in = self.sem(ctx, "later_in")

    def table_buffers(self, c):
        self.whole = {k: self.sb(c, k, [EXPERTS, F1 * D1]) for k in TABLES}
        self.mid = self.sb(c, "mid", [EXPERTS, F1 * D1], BF16)
        self.table_in = [self.sem(c, "table_in") for _ in TABLES]
        self.split_link, self.mid_done, self.mid_moved = (self.sem(c, n) for n in ("split_link", "mid_done", "mid_moved"))


    def load_constants(self, act, const):
        a = self.a
        for n, k in enumerate(("bq", "bk", "bv")):
            act.dma_start(self.b_qkv[:, n * D:(n + 1) * D], a["L0_attn_a_" + k].partition_broadcast(P)).then_inc(const, 16)
        act.dma_start(self.ln_g[:], a["L0_attn_a_ln_g"].rearrange("(p o) -> p o", o=1)).then_inc(const, 16)
        act.dma_start(self.ln_b[:], a["L0_attn_a_ln_b"].rearrange("(p o) -> p o", o=1)).then_inc(const, 16)
        act.dma_start(self.b_qkv_b[:], a["L0_attn_b_qkv_bias"][0].partition_broadcast(P)).then_inc(const, 16)
        act.dma_start(self.scale_up[:], a["L0_ffn_scale_up"].partition_broadcast(P)).then_inc(const, 16)
        act.dma_start(self.scale_dn[:], a["L0_ffn_scale_down"].partition_broadcast(P)).then_inc(const, 16)
        for half in range(2):
            act.dma_start(self.bias_up[64 * half:64 * half + 64, :],
                          a["L0_ffn_bias_up"].rearrange("(o p) -> o p", p=F1)).then_inc(const, 16)
        return 10 * 16

    def make_constants(self, pool, chain):
        nc = self.nc
        nc.gpsimd.memset(self.half_neg[:], -0.5).then_inc(chain, 1)
        nc.gpsimd.memset(self.ident[:], 0.0).then_inc(chain, 1)
        nc.gpsimd.memset(self.identb[:], 0.0).then_inc(chain, 1)
        nc.gpsimd.memset(self.mask_qk[:], 0.0).then_inc(chain, 1)
        nc.gpsimd.memset(self.mask_kq[:], 0.0).then_inc(chain, 1)
        nc.gpsimd.iota(self.iota_e[:], pattern=[[0, 2], [1, EXPERTS]], base=0, channel_multiplier=0,
                       allow_small_or_imprecise_dtypes=True).then_inc(chain, 1)
        pool.wait_ge(chain, 6)
        for m in (self.ident, self.identb):
            nc.gpsimd.affine_select(out=m[:], in_=m[:], pattern=[[-1, P]], compare_op=ALU.not_equal,
                                    fill=1.0, base=0, channel_multiplier=1).then_inc(chain, 1)
        nc.gpsimd.affine_select(out=self.mask_qk[:], in_=self.mask_qk[:], pattern=[[-1, P]],
                                compare_op=ALU.is_ge, fill=MASKED, base=0, channel_multiplier=1).then_inc(chain, 1)
        nc.gpsimd.affine_select(out=self.mask_kq[:], in_=self.mask_kq[:], pattern=[[1, P]],
                                compare_op=ALU.is_ge, fill=MASKED, base=0, channel_multiplier=-1).then_inc(chain, 1)
        nc.gpsimd.memset(self.ones[:], 1.0).then_inc(chain, 1)

    def keep_clock(self, b, n, moving):
        for _ in range(n):
            self.nc.tensor.matmul(b[:, 0:moving.shape[-1]], self.identb[:], moving, start=True, stop=True)

    def layernorm_dve(self, dve, src, dst, s, loaded=None):
        nc = self.nc
        for c in range(CHUNKS + 2):
            if c < CHUNKS:
                if loaded:
                    dve.wait_ge(loaded[c], 16)
                for t in range(CH * c, CH * c + CH):
                    nc.vector.bn_stats(s["stats"][:, t, :], src[:, t, :]).then_inc(s["stat_done"], 1)
            if 1 <= c <= CHUNKS:
                dve.wait_ge(s["stat_done"], CH * c)
                for t in range(CH * c - CH, CH * c):
                    nc.vector.bn_aggr(s["meanvar"][:, t, :], s["stats"][:, t, :]).then_inc(s["aggr_done"], 1)
            if c >= 2:
                dve.wait_ge(s["rstd_done"], c - 1)
                for t in range(CH * (c - 2), CH * (c - 1)):
                    nc.vector.tensor_scalar(dst[:, t, :], src[:, t, :], s["meanvar"][:, t, 0:1], s["rstd"][:, t:t + 1],
                                            ALU.subtract, ALU.mult).then_inc(s["normed"], 1)

    def layernorm_pool(self, pool, s, twice=False):
        nc = self.nc
        for c in range(CHUNKS):
            rstd = s["rstd"][:, CH * c:CH * c + CH]
            pool.wait_ge(s["aggr_done"], CH * (c + 1))
            nc.gpsimd.tensor_scalar(rstd, s["meanvar"][:, CH * c:CH * c + CH, 1], 1.0 + EPS if twice else 1.0,
                                    EPS * EPS if twice else EPS, ALU.mult, ALU.add).then_inc(s["eps_added"], 1)
            pool.wait_ge(s["eps_added"], c + 1)
            nc.gpsimd.tensor_tensor(rstd, rstd, self.half_neg[:, 0:CH], ALU.pow).then_inc(s["rstd_done"], 1)

    def layernorm_state(self, c):
        s = {n: self.sem(c, n) for n in ("stat_done", "aggr_done", "eps_added", "rstd_done", "normed")}
        s["stats"] = self.sb(c, "stats", [P, TILES, 6])
        s["meanvar"] = self.sb(c, "meanvar", [P, TILES, 2])
        s["rstd"] = self.sb(c, "rstd", [P, TILES])
        return s

    def build_stack(self, eng, ops, stack, src, rest, keys, link, links, built):
        his, mids, lo = ((1, 4, 6), (2, 5), 3) if keys else ((1, 2, 3), (4, 5), 6)
        part = lambda k: stack[:, :, :, :, 8 * k:8 * k + 8].rearrange("p u t h e -> p (u t h) e")
        n = [0]

        def chained(ins, wait=True):
            ins.then_inc(link, 1)
            n[0] += 1
            if wait:
                eng.wait_ge(link, links + n[0])

        chained(ops.tensor_copy(part(his[0]), src))
        for k in his[1:]:
            chained(ops.tensor_copy(part(k), part(his[0])), wait=False)
        chained(ops.tensor_tensor(rest[:], src, part(his[0]), ALU.subtract))
        chained(ops.tensor_copy(part(mids[0]), rest[:]))
        chained(ops.tensor_copy(part(mids[1]), part(mids[0])), wait=False)
        chained(ops.tensor_tensor(rest[:], rest[:], part(mids[0]), ALU.subtract))
        ops.tensor_copy(part(lo), rest[:]).then_inc(built, 1)
        return n[0]

    def attention_inputs(self, c):
        self.q_stack = [self.sb(c, "q_stack", [P, 2, TPB, 2, STACK], BF16) for _ in range(2)]
        self.k_stack = [self.sb(c, "k_stack", [P, 2, TPB, 2, STACK], BF16) for _ in range(2)]
        self.v_aug = [self.sb(c, "v_aug", [P, 2, TPB, 2, 32]) for _ in range(2)]
        self.rest = self.sb(c, "rest", [P, 4 * TPB, HD])
        self.qkv_back = [self.sem(c, "qkv_back") for _ in range(QUADS)]

    def blank_inputs(self, pool, blank, done):
        nc = self.nc
        for b in range(2):
            nc.gpsimd.memset(self.k_stack[b][:], 0.0).then_inc(blank, 1)
            nc.gpsimd.memset(self.q_stack[b][:], 0.0).then_inc(blank, 1)
            nc.gpsimd.memset(self.v_aug[b][:], 0.0).then_inc(blank, 1)
        pool.wait_ge(blank, done + 6)
        for b in range(2):
            nc.gpsimd.memset(self.k_stack[b][:, :, :, :, 0:2], 1.0).then_inc(blank, 1)
            nc.gpsimd.memset(self.v_aug[b][:, :, :, :, HD:HD + 1], 1.0).then_inc(blank, 1)

    def values_of(self, qkv, i, par):
        return (self.v_aug[par][:, :, :, :, 0:HD].rearrange("p u t h e -> p (u t h) e"), qkv[:, i, :, 2 * HD:3 * HD])

    def project(self, causal, qkv):
        nc, a = self.nc, self.a
        first = not causal
        with ExitStack() as c:
            sb, sem = self.sb, self.sem
            xn = sb(c, "xn", [P, TILES, D])
            xt = sb(c, "xt", [P, TILES, P])
            rest_k = sb(c, "rest_k", [P, 4 * TPB, HD])
            rows = sb(c, "rows", [P, TILES, 3 * D]) if causal else None
            if first:
                wu = sb(c, "wu", [EXPERTS, D1 * D1])
                wd = sb(c, "wd", [EXPERTS, F1 * F1])
                bd = sb(c, "bd", [D1, D1])
            s = self.layernorm_state(c)
            bank = self.banks(c)
            filled, by_dve, by_act = (sem(c, n) for n in ("filled", "by_dve", "by_act"))
            x_in = [sem(c, "x_in") for _ in range(CHUNKS)] if first else None
            w_in, routers_in, const = (sem(c, n) for n in ("w_in", "routers_in", "const"))
            k_link, q_link, k_built, q_built, v_built = (
                sem(c, n) for n in ("k_link", "q_link", "k_built", "q_built", "v_built"))
            stored = [sem(c, "stored") for _ in range(QUADS)] if causal else None
            block = c.enter_context(nc.Block())
            blanked = CONSTANTS + (2 if causal else 1) * BLANKS
            w = self.w_qkv_b if causal else self.w_qkv
            bias = self.b_qkv_b if causal else self.b_qkv

            ROUTERS = 1 + F1 // 8 + 1 if first else 0
            BURST, BURST_END = (0, 0) if first else (50, 100)
            FIRST_QUAD = TPB if first else 0

            @block.tensor
            def _(pe):
                pe.wait_ge(self.made, 8)
                self.keep_clock(bank[0], BURST, self.identb[:])
                for j in range(CHUNKS):
                    for t in range(CH * j, CH * j + CH):
                        pe.wait_ge(s["normed"], t + 1)
                        ins = nc.tensor.transpose(bank[j][:, (t % CH) * P:(t % CH + 1) * P], xn[:, t, :], self.ident[:])
                    ins.then_inc(filled, 1)
                if first:
                    pe.wait_ge(w_in, 3 * 16)
                for t in range(TILES):
                    if t % CH == 0:
                        pe.wait_ge(by_act, t // CH + 1)
                    if t >= 4:
                        pe.wait_ge(by_dve, t - 3)
                    nc.tensor.matmul(bank[4 + t % 4][:, 0:3 * D], xt[:, t, :], w[:], start=True,
                                     stop=True).then_inc(filled, 1)
                self.keep_clock(bank[0], BURST_END, self.identb[:])
                for j in range(ROUTERS):
                    b = bank[j % 4]
                    if j == 0:
                        pe.wait_ge(routers_in, 3 * 16)
                        for r in range(TOKROWS):
                            ins = nc.tensor.transpose(b[:, r * 64:(r + 1) * 64], wu[:, r * D:(r + 1) * D],
                                                      self.ident[0:64, 0:64])
                    elif j < ROUTERS - 1:
                        if j >= 4:
                            pe.wait_ge(by_act, CHUNKS + j - 3)
                        wd_by_p = wd[:].rearrange("e (o p) -> e p o", p=F1)
                        for p in range(8):
                            ins = nc.tensor.matmul(b[0:64, p * 64:(p + 1) * 64], wd_by_p[:, 8 * (j - 1) + p, :],
                                                   self.ident[0:64, 0:64], start=True, stop=True)
                    else:
                        pe.wait_ge(by_act, CHUNKS + j - 3)
                        for g in range(4):
                            ins = nc.tensor.matmul(b[32 * g:32 * g + 32, 0:D1], bd[:], self.ident[0:32, 0:32],
                                                   start=True, stop=True)
                    ins.then_inc(filled, 1)

            @block.scalar
            def _(act):
                if first:
                    total = self.load_constants(act, const)
                for j in range(CHUNKS):
                    act.wait_ge(filled, j + 1)
                    dst = xt[:, CH * j:CH * j + CH, :].rearrange("p t r -> p (t r)")
                    if causal:
                        nc.scalar.activation(dst, bank[j][:], ACT.Identity).then_inc(by_act, 1)
                    else:
                        if j == 0:
                            act.wait_ge(const, total)
                        nc.scalar.activation(dst, bank[j][:], ACT.Identity, bias=self.ln_b[:],
                                             scale=self.ln_g[:]).then_inc(by_act, 1)
                act.wait_ge(*((self.qkv_back[0], 4 * 16) if causal else (by_dve, FIRST_QUAD)))
                act.wait_ge(self.made, blanked)
                dst, src = self.values_of(qkv, 0, 0)
                nc.scalar.activation(dst, src, ACT.Copy).then_inc(v_built, 1)
                for j in range(ROUTERS):
                    act.wait_ge(filled, CHUNKS + TILES + j + 1)
                    b = bank[j % 4]
                    if j == 0:
                        dst, src = self.router_up[:].rearrange("p r e -> p (r e)"), b[:]
                    elif j < ROUTERS - 1:
                        dst, src = self.router_dn[0:64, 8 * (j - 1):8 * j, :].rearrange("p o e -> p (o e)"), b[0:64, :]
                    else:
                        dst, src = self.bias_dn[:], b[:, 0:D1]
                    nc.scalar.activation(dst, src, ACT.Copy).then_inc(by_act, 1)

            @block.gpsimd
            def _(pool):
                if first:
                    self.make_constants(pool, self.made)
                self.layernorm_pool(pool, s, twice=first)
                self.blank_inputs(pool, self.made, blanked - BLANKS)
                pool.wait_ge(*((self.qkv_back[0], 4 * 16) if causal else (by_dve, FIRST_QUAD)))
                pool.wait_ge(self.made, blanked)
                self.build_stack(pool, nc.gpsimd, self.q_stack[0], qkv[:, 0, :, 0:HD], self.rest, False, q_link, 0, q_built)

            @block.vector
            def _(dve):
                self.layernorm_dve(dve, self.x, xn, s, loaded=x_in)
                if first:
                    dve.wait_ge(const, 10 * 16)
                for t in range(TILES):
                    dve.wait_ge(filled, CHUNKS + t + 1)
                    src = bank[4 + t % 4][:, 0:3 * D]
                    if causal:
                        nc.vector.tensor_tensor(rows[:, t, :], src, bias[:], ALU.add).then_inc(by_dve, 1)
                    else:
                        b, tt = t // TPB, t % TPB
                        half = qkv[:, 4 * b:4 * b + 4].rearrange("p q (u t h) e -> p (q u) t h e", u=2, h=2)
                        for n in range(3):
                            cut = lambda v: v.rearrange("p (s u h e) -> p s u h e", s=3, h=2, e=HD)[:, n]
                            ins = nc.vector.tensor_tensor(half[:, :, tt, :, n * HD:(n + 1) * HD], cut(src),
                                                          cut(bias[:]), ALU.add)
                        ins.then_inc(by_dve, 1)
                    if t == (TILES - 4 if causal else TPB + 1):
                        dve.wait_ge(*((self.qkv_back[0], 4 * 16) if causal else (by_dve, FIRST_QUAD)))
                        dve.wait_ge(self.made, blanked)
                        self.build_stack(dve, nc.vector, self.k_stack[0], qkv[:, 0, :, HD:2 * HD], rest_k, True,
                                         k_link, 0, k_built)

            @block.sync
            def _(sp):
                if first:
                    x_rows = a["L0_attn_a_x"].rearrange("b (t p) d -> p (b t) d", p=P)
                    for j in range(CHUNKS):
                        sp.dma_start(self.x[:, CH * j:CH * j + CH, :], x_rows[:, CH * j:CH * j + CH, :]).then_inc(x_in[j], 16)
                    sp.dma_start(wu[:], a["L0_ffn_W_up"]).then_inc(routers_in, 16)
                    sp.dma_start(wd[:], a["L0_ffn_W_down"]).then_inc(routers_in, 16)
                    sp.dma_start(bd[:], a["L0_ffn_bias_down"].rearrange("(o p) -> o p", p=D1)).then_inc(routers_in, 16)
                    for n, k in enumerate(("Wq", "Wk", "Wv")):
                        sp.dma_start(self.w_qkv[:, n * D:(n + 1) * D], a["L0_attn_a_" + k]).then_inc(w_in, 16)
                    sp.dma_start(self.w_qkv_b[:], a["L0_attn_b_qkv_kernel"]).then_inc(self.later_in, 16)
                    for n, k in enumerate(TABLES):
                        sp.dma_start(self.whole[k][:], a["L0_ffn_" + k].rearrange("e o i -> e (o i)")) \
                          .then_inc(self.table_in[n], 16)
                    sp.wait_ge(by_act, CHUNKS + ROUTERS)
                    sp.dma_start(self.router_dn[64:P], self.router_dn[0:64]).then_inc(self.later_in, 16)
                    sp.wait_ge(w_in, 3 * 16)
                else:
                    per = TILES // QUADS
                    by_row = self.scratch_qkv.rearrange("(t p) f -> p t f", p=P)
                    for i in range(QUADS):
                        sp.wait_ge(by_dve, per * (i + 1))
                        sp.dma_start(by_row[:, per * i:per * i + per, :], rows[:, per * i:per * i + per, :]) \
                          .then_inc(stored[i], 16)
                        if i == 1:
                            sp.wait_ge(stored[0], 16)
                            self.load_quad(sp, qkv, 0)
                    for i in range(1, QUADS):
                        sp.wait_ge(stored[i], 16)

    def load_quad(self, sp, qkv, i):
        by_pos = self.scratch_qkv.rearrange("r (c f) -> (r c) f", f=24).rearrange("(i n p) f -> p i n f", p=P, i=QUADS)
        dst = qkv[:, i].rearrange("p (u t h) f -> p u h t f", u=2, h=2)
        for g in range(4):
            sp.dma_start(dst[:, g // 2, g % 2], by_pos[:, i, g * TPB:(g + 1) * TPB]).then_inc(self.qkv_back[i], 16)

    def split_table(self, pool, n, count):
        nc = self.nc
        k = TABLES[n]
        whole = self.whole[k]
        pool.wait_ge(self.table_in[n], 16)
        nc.gpsimd.tensor_copy(self.tab_hm[k][0:EXPERTS, :], whole[:]).then_inc(self.split_link, 1)
        pool.wait_ge(self.split_link, count + 1)
        nc.gpsimd.tensor_tensor(whole[:], whole[:], self.tab_hm[k][0:EXPERTS, :], ALU.subtract).then_inc(self.split_link, 1)
        pool.wait_ge(self.split_link, count + 2)
        if n:
            pool.wait_ge(self.mid_moved, 16 * n)
        nc.gpsimd.tensor_copy(self.mid[:], whole[:]).then_inc(self.mid_done, 1)
        pool.wait_ge(self.mid_done, n + 1)
        nc.gpsimd.tensor_tensor(self.tab_lo[k][0:EXPERTS, :], whole[:], self.mid[:], ALU.subtract).then_inc(self.split_link, 1)
        pool.wait_ge(self.split_link, count + 3)
        nc.gpsimd.memset(self.tab_lo[k][EXPERTS:P, :], 0.0).then_inc(self.split_link, 1)
        pool.wait_ge(self.split_link, count + 4)
        return count + 4

    def attention(self, causal, qkv, y):
        nc = self.nc
        scale = 1.0 / (2.0 * D) ** 0.5 if causal else 1.0 / HD ** 0.5
        with ExitStack() as c:
            sb, sem = self.sb, self.sem
            q_stack, k_stack, v_aug, rest = self.q_stack, self.k_stack, self.v_aug, self.rest
            kt = [sb(c, "kt", [P, 2, SEQ], BF16) for _ in range(2)]
            qt_max = sb(c, "qt_max", [P, 2, SEQ], BF16)
            qt = [sb(c, "qt", [P, 2, SEQ], BF16) for _ in range(2)]
            mx = sb(c, "mx", [P, 2, TPB, 2])
            NP = 8
            probs = sb(c, "probs", [P, NP, BANK])
            ysum = sb(c, "ysum", [P, BANK])
            yrec = sb(c, "yrec", [P, 2, 4, 4])
            self.names += 1
            unit = [c.enter_context(nc.psum_tensor(f"unit{u}_{self.names}", [P, 2 * BANK], F32)) for u in range(2)]
            score = [c.enter_context(nc.psum_tensor(f"score{u}_{self.names}", [P, BANK], F32)) for u in range(3)]
            weighted = c.enter_context(nc.psum_tensor(f"weighted_{self.names}", [P, BANK], F32))

            link, k_built, q_built, v_built = (sem(c, n) for n in ("link", "k_built", "q_built", "v_built"))
            unit_filled, unit_done = sem(c, "unit_filled"), sem(c, "unit_done")
            shift_link, shift_ready = sem(c, "shift_link"), sem(c, "shift_ready")
            scores_ready, probs_ready, probs_used = (sem(c, n) for n in ("scores_ready", "probs_ready", "probs_used"))
            sum_copied, norm_link = sem(c, "sum_copied"), sem(c, "norm_link")
            y_stored = [sem(c, "y_stored") for _ in range(QUADS)] if causal else None
            y_back = [sem(c, "y_back") for _ in range(QUADS)] if causal else None
            added = sem(c, "added")
            rows = sb(c, "yrows", [P, TILES, D]) if causal else None
            block = c.enter_context(nc.Block())

            SLOTS = [(qh, kb, max(0, kb * P - qh * BANK) if causal else 0) for qh in range(2) for kb in range(TPB)
                     if not causal or kb * P < (qh + 1) * BANK]
            NS = len(SLOTS)
            UNITS = 4 * NS
            HALF0 = sum(qh == 0 for qh, _, _ in SLOTS)
            diag = lambda qh, kb: causal and kb * P >= qh * BANK

            BURST = 8
            SPREAD = 0.94 if causal else 0.98
            PREP = [("k", 0), ("q", 0), ("k", 1), ("q", 1)]
            PREP += [("max", 0, t, g) for t in range(TPB) for g in range(2)]
            PREP += [("max", 1, t, g) for t in range(2) for g in range(2)]
            PREP += [("shifted", 0)]
            PREP += [("max", 1, t, g) for t in range(2, TPB) for g in range(2)]
            PREP += [("shifted", 1)]
            NPREP = len(PREP)
            JOBS = NPREP + 2

            def columns(job):
                return {"max": 80 + ((job[2] + 1) * P if causal else SEQ) if job[0] == "max" else 0,
                        "y": 500}.get(job[0], 80 + SEQ // 2)

            def step_jobs(first, prep, last):
                by_place = [[] for _ in range(2 * NS + 1)]
                if prep:
                    jobs = PREP[:-1] + [("y", 0)] + PREP[-1:]
                    whole = sum(map(columns, jobs))
                    reach = sum(BANK - off for _, _, off in SLOTS)
                    ends, done = [], 0
                    for _, _, off in SLOTS:
                        for _ in range(2):
                            done += (BANK - off) / 2
                            ends.append(done / reach)
                    spent = 0
                    for job in jobs:
                        at = spent / whole * SPREAD
                        by_place[next(k for k, e in enumerate(ends) if e > at)].append(job)
                        spent += columns(job)
                else:
                    by_place[2 * (HALF0 + 2)].append(("y", 0))
                if not first:
                    by_place[4].insert(0, ("y", 1))
                if last:
                    by_place[2 * NS].append(("y", 1))
                return by_place

            def jobs_before(i):
                return NPREP if type(i) is int and i == 0 else JOBS * i + NPREP - 1

            def job_parity(i):
                return NPREP % 2 if type(i) is int and i == 0 else (NPREP - 1) % 2
            assert JOBS % 2 == 0

            def same_bank_before(u):
                if u >= 3:
                    return 3
                return next(UNITS - v for v in range(UNITS - 1, -1, -1) if v % 3 == u) + u

            flat = [job for jobs in step_jobs(False, True, False) for job in jobs]
            Y1_AT, Y0_AT = flat.index(("y", 1)), flat.index(("y", 0))

            def quad_summed(eng, i):
                if i < QUADS - 1:
                    eng.wait_ge(unit_done, jobs_before(i + 1) + (Y1_AT if i < QUADS - 2 else 0) + 1)
                else:
                    eng.wait_ge(unit_done, JOBS * QUADS)

            def build(pool, i, links):
                par = i % 2
                if causal:
                    pool.wait_ge(self.qkv_back[i], 4 * 16)
                if i >= 2:
                    pool.wait_ge(unit_filled, JOBS * i - 2 * JOBS + NPREP)
                n = self.build_stack(pool, nc.gpsimd, k_stack[par], qkv[:, i, :, HD:2 * HD], rest, True, link, links, k_built)
                pool.wait_ge(k_built, i)
                n += self.build_stack(pool, nc.gpsimd, q_stack[par], qkv[:, i, :, 0:HD], rest, False, link, links + n,
                                      q_built)
                if i >= 2:
                    pool.wait_ge(probs_used, UNITS * i - UNITS)
                dst, src = self.values_of(qkv, i, par)
                nc.gpsimd.tensor_copy(dst, src).then_inc(v_built, 1)
                pool.wait_ge(q_built, i)
                return n

            def add_residual(pool, i):
                if causal:
                    pool.wait_ge(y_back[i], 16)
                    xv = self.x[:, 2 * i:2 * i + 2, :]
                    nc.gpsimd.tensor_tensor(xv, xv, rows[:, 2 * i:2 * i + 2, :], ALU.add).then_inc(added, 1)
                else:
                    quad_summed(pool, i)
                    b, q = i // 4, i % 4
                    xv = self.x[:, b * TPB:(b + 1) * TPB, 32 * q:32 * q + 32].rearrange("p t (g e) -> p t g e", g=4)
                    yv = y[:, i].rearrange("p g t e -> p t g e")
                    nc.gpsimd.tensor_tensor(xv, xv, yv, ALU.add).then_inc(added, 1)

            @block.gpsimd
            def _(pool):
                links = split = 0
                for i in range(1, QUADS):
                    links += build(pool, i, links)
                    if not causal and 0 <= i - 2 < len(TABLES):
                        split = self.split_table(pool, i - 2, split)
                    if i >= 3:
                        add_residual(pool, i - 3)
                for i in range(QUADS - 3, QUADS):
                    add_residual(pool, i)

            def scores_of(pe, i, par, slot, first, heads):
                qh, kb, off = SLOTS[slot]
                for g in heads:
                    u = 4 * slot + g
                    back = same_bank_before(u)
                    if not (first and u < 3):
                        pe.wait_ge(probs_ready, i * UNITS + (u - back + 1))
                    rows = slice(64 * (g % 2), 64 * (g % 2) + STACK_USED)
                    out = score[u % 3]
                    ins = nc.tensor.matmul(out[:, off:BANK], kt[par][rows, g // 2, kb * P:kb * P + P],
                                           qt[par][rows, g // 2, qh * BANK + off:(qh + 1) * BANK],
                                           start=True, stop=not diag(qh, kb))
                    if diag(qh, kb):
                        ins = nc.tensor.matmul(out[:, off:off + P], self.identb[:], self.mask_kq[:],
                                               start=False, stop=True)
                    ins.then_inc(scores_ready, 1)

            def weigh(pe, i, par, slot, first):
                qh, kb, off = SLOTS[slot]
                if slot == 0:
                    if not first:
                        pe.wait_ge(v_built, i)
                        pe.wait_ge(sum_copied, 2 * i)
                if slot == HALF0:
                    pe.wait_ge(sum_copied, 2 * i + 1)
                for g in range(4):
                    u = 4 * slot + g
                    pe.wait_ge(probs_ready, i * UNITS + u + 1)
                    nc.tensor.matmul(weighted[32 * g:32 * g + 32, off:BANK], v_aug[par][:, g // 2, kb, g % 2, :],
                                     probs[:, u % NP, off:BANK], start=kb == 0,
                                     stop=slot in (HALF0 - 1, NS - 1)).then_inc(probs_used, 1)

            def unit_job(pe, job, number, static_number, i_prep, par_prep, i):
                ubuf = unit[static_number % 2]
                if not (type(number) is int and number < 2):
                    pe.wait_ge(unit_done, number - 1)
                kind = job[0]
                prologue = type(number) is int and number < NPREP
                if kind in ("k", "q", "shifted"):
                    pair = job[1]
                    if kind == "k":
                        if not prologue:
                            pe.wait_ge(k_built, i_prep)
                        src = k_stack[par_prep]
                    else:
                        src = q_stack[par_prep]
                        if kind == "q" and not prologue:
                            pe.wait_ge(q_built, i_prep)
                        if kind == "shifted":
                            if prologue and pair == 1:
                                self.keep_clock(ubuf, BURST, kt[0][:, 0, 0:BANK])
                            pe.wait_ge(shift_ready, 2 * i_prep + pair + 1)
                    dst = ubuf[:].bitcast(BF16)
                    for t in range(TPB):
                        ins = nc.tensor.transpose(dst[:, t * P:(t + 1) * P], src[:, pair, t, :, :].rearrange("p h k -> p (h k)"),
                                                  self.identb[:])
                elif kind == "max":
                    _, pair, t, g = job
                    if t == 0 and g == 0:
                        pe.wait_ge(unit_done, number - max_since[pair])
                    rows = slice(64 * g, 64 * g + STACK_USED)
                    width = (t + 1) * P if causal else SEQ
                    for h in range(0, width, BANK):
                        end = min(h + BANK, width)
                        on_diag = causal and end == width
                        ins = nc.tensor.matmul(ubuf[:, h:end], qt_max[rows, pair, t * P:t * P + P],
                                               kt[par_prep][rows, pair, h:end], start=True, stop=not on_diag)
                        if on_diag:
                            ins = nc.tensor.matmul(ubuf[:, width - P:width], self.identb[:], self.mask_qk[:],
                                                   start=False, stop=True)
                else:
                    half = job[1]
                    pe.wait_ge(sum_copied, 2 * i + half + 1)
                    for t in range(4):
                        ins = nc.tensor.transpose(ubuf[:, t * P:(t + 1) * P], ysum[:, t * P:(t + 1) * P], self.ident[:])
                ins.then_inc(unit_filled, 1)

            max_since = {p: PREP.index(("max", p, 0, 0)) - PREP.index(("q", p)) - 1 for p in range(2)}

            def walk(i, first, prep, last):
                n = 0
                for place, jobs in enumerate(step_jobs(first, prep, last)):
                    for job in jobs:
                        quad = i + 1
                        if job[0] == "y":
                            quad = i - 1 if job[1] == 1 and place < 2 * NS else i
                        yield place, job, jobs_before(i) + n, job_parity(i) + n, quad
                        n += 1

            def pe_step(pe, i, par, first=False, prep=True, last=False):
                jobs = list(walk(i, first, prep, last))

                def jobs_at(place):
                    for at, job, number, static, quad in jobs:
                        if at == place:
                            unit_job(pe, job, number, static, quad, 1 - par, quad)

                pe.wait_ge(unit_done, jobs_before(i))
                for slot in range(NS):
                    scores_of(pe, i, par, slot, first, (0, 1))
                    jobs_at(2 * slot)
                    scores_of(pe, i, par, slot, first, (2, 3))
                    if slot:
                        weigh(pe, i, par, slot - 1, first)
                    elif not first:
                        weigh(pe, i - 1, 1 - par, NS - 1, False)
                    jobs_at(2 * slot + 1)
                if last:
                    weigh(pe, i, par, NS - 1, first)
                    jobs_at(2 * NS)

            def drive(engine, step):
                step(engine, 0, 0, first=True)
                with engine.Fori(1, QUADS - 1, 2) as i:
                    step(engine, i, 1)
                    step(engine, i + 1, 0)
                step(engine, QUADS - 1, 1, prep=False, last=True)

            @block.tensor
            def _(pe):
                for n, job in enumerate(PREP):
                    unit_job(pe, job, n, n, 0, 0, 0)
                drive(pe, pe_step)


            def copy_sums(act, i, half, first=False, alone=False):
                act.wait_ge(probs_used, i * UNITS + (UNITS if half else 4 * HALF0))
                if half:
                    act.wait_ge(unit_filled, jobs_before(i) + 2 if alone else JOBS * i + NPREP + Y0_AT)
                elif not first:
                    act.wait_ge(unit_filled, jobs_before(i) + (0 if alone else Y1_AT) + 1)
                nc.scalar.activation(ysum[:], weighted[:], ACT.Copy).then_inc(sum_copied, 1)

            def act_step(act, i, par, first=False, prep=True, last=False):
                for slot in range(NS):
                    qh, kb, off = SLOTS[slot]
                    for g in range(4):
                        u = 4 * slot + g
                        act.wait_ge(scores_ready, i * UNITS + u + 1)
                        if not (first and u < NP):
                            act.wait_ge(probs_used, i * UNITS + (u - NP + 1))
                        nc.scalar.activation(probs[:, u % NP, off:BANK], score[u % 3][:, off:BANK], ACT.Exp,
                                             scale=scale).then_inc(probs_ready, 1)
                        if slot == 1 and g == 1 and not first:
                            copy_sums(act, i - 1, 1)
                        if slot == HALF0 + 1 and g == 1:
                            copy_sums(act, i, 0, first, not prep)
                if last:
                    copy_sums(act, i, 1, alone=True)

            @block.scalar
            def _(act):
                drive(act, act_step)

            def dve_job(dve, job, number, static_number, par_prep, quad):
                ubuf = unit[static_number % 2]
                dve.wait_ge(unit_filled, number + 1)
                kind = job[0]
                if kind in ("k", "q", "shifted"):
                    pair = job[1]
                    dst = {"k": kt[par_prep], "q": qt_max, "shifted": qt[par_prep]}[kind]
                    nc.vector.tensor_copy(dst[:, pair, :], ubuf[:].bitcast(BF16)[:, 0:SEQ]).then_inc(unit_done, 1)
                elif kind == "max":
                    _, pair, t, g = job
                    width = (t + 1) * P if causal else SEQ
                    nc.vector.reduce_max(mx[:, pair, t, g:g + 1], ubuf[:, 0:width], AXX).then_inc(unit_done, 1)
                    if t == TPB - 1 and g == 1:
                        dve.wait_ge(unit_done, number + 1)
                        m = mx[:, pair].rearrange("p t h -> p (t h)")
                        hi = q_stack[par_prep][:, pair, :, :, 0].rearrange("p t h -> p (t h)")
                        lo = q_stack[par_prep][:, pair, :, :, 1].rearrange("p t h -> p (t h)")
                        nc.vector.tensor_scalar(hi, m, -1.0, None, ALU.mult).then_inc(shift_link, 1)
                        dve.wait_ge(shift_link, 2 * quad + pair + 1)
                        nc.vector.scalar_tensor_tensor(out=lo, in0=m, scalar=-1.0, in1=hi, op0=ALU.mult,
                                                       op1=ALU.subtract).then_inc(shift_ready, 1)
                else:
                    half = job[1]
                    sums = ubuf[:, 0:BANK].rearrange("p (t g e) -> p t g e", t=4, g=4)
                    nc.vector.reciprocal(yrec[:, half], sums[:, :, :, HD]).then_inc(norm_link, 1)
                    dve.wait_ge(norm_link, 2 * quad + half + 1)
                    dst = y[:, quad, :, 4 * half:4 * half + 4, :].rearrange("p g t e -> p t g e")
                    rec = yrec[:, half].unsqueeze(3).broadcast_to([P, 4, 4, HD])
                    nc.vector.tensor_tensor(dst, sums[:, :, :, 0:HD], rec, ALU.mult).then_inc(unit_done, 1)

            def dve_step(dve, i, par, first=False, prep=True, last=False):
                for s, job, number, static, quad in walk(i, first, prep, last):
                    dve_job(dve, job, number, static, 1 - par, quad)

            @block.vector
            def _(dve):
                for n, job in enumerate(PREP):
                    dve_job(dve, job, n, n, 0, 0)
                drive(dve, dve_step)

            @block.sync
            def _(sp):
                if causal:
                    by_pos = self.scratch_y.rearrange("(i n p e) -> p i n e", i=QUADS, p=P, e=HD)
                    for i in range(1, QUADS):
                        self.load_quad(sp, qkv, i)
                    by_row = self.scratch_y.rearrange("(t p d) -> p t d", p=P, d=D)
                    for i in range(QUADS):
                        quad_summed(sp, i)
                        sp.dma_start(by_pos[:, i], y[:, i].rearrange("p g t e -> p (g t) e")).then_inc(y_stored[i], 16)
                        sp.wait_ge(y_stored[i], 16)
                        sp.dma_start(rows[:, 2 * i:2 * i + 2, :], by_row[:, 2 * i:2 * i + 2, :]).then_inc(y_back[i], 16)
                else:
                    for n, k in enumerate(TABLES):
                        sp.wait_ge(self.mid_done, n + 1)
                        sp.dma_start(self.tab_hm[k][EXPERTS:P, :], self.mid[:]).then_inc(self.mid_moved, 16)
                        sp.wait_ge(self.mid_moved, 16 * (n + 1))
                    sp.wait_ge(self.later_in, 2 * 16)

    def mixture(self, final):
        nc = self.nc
        NT = 16
        with ExitStack() as c:
            sb, sem = self.sb, self.sem
            tok = sb(c, "tok", [P, 4 * NT, D1])
            fa = sb(c, "fa", [P, 8192])
            fb = sb(c, "fb", [P, 8192])
            diag = sb(c, "diag", [P, 2, 2048])
            hid = sb(c, "hid", [P, P, F1])
            xn = hid[:, 0:32, :].rearrange("p (t a) d -> p t (a d)", t=TILES)
            xt = hid[:, 32:64, :].rearrange("p (t a) r -> p t (a r)", t=TILES)
            staged = hid[:].rearrange("p m q -> p (m q)").rearrange("p (j n) -> p j n", j=16)
            yt = tok[:].rearrange("p n i -> p (n i)").rearrange("p (d n o) -> p d n o", d=2, o=D1)
            logit_t = sb(c, "logit_t", [P, P])
            logit = sb(c, "logit", [P, 2, EXPERTS])
            top = sb(c, "top", [P, 2, 8])
            index = sb(c, "index", [P, 2, 8], U32)
            indexf = sb(c, "indexf", [P, 2, 2])
            gap = sb(c, "gap", [P, 4, 2])
            one_w = sb(c, "one_w", [P, 2, 2, EXPERTS])
            one_b = sb(c, "one_b", [P, 2, 2, 2 * EXPERTS], BF16)
            pick = sb(c, "pick", [P, 2, 512], BF16)
            pick_w = sb(c, "pick_w", [EXPERTS, 512])
            weight = sb(c, "weight", [P, 512])
            s = self.layernorm_state(c)
            bank = self.banks(c)
            filled, by_dve, by_act = sem(c, "filled"), sem(c, "by_dve"), sem(c, "by_act")
            top_link, exp_ready, gelu_done, zeroed = (sem(c, n) for n in ("top_link", "exp_ready", "gelu_done", "zeroed"))
            stored, moved = sem(c, "stored"), sem(c, "moved")
            block = c.enter_context(nc.Block())
            fa_up = fa[:].rearrange("p (o n) -> p o n", o=F1)
            MOVES = 2

            BUSY = {"start": 26, "first_up": 8, "moved": 12, "first_down": 16, "gelu": 16, "logits": 2, "pick": 30}

            JOBS = [("xt", j) for j in range(4)] + [("logits", 0), ("tok", 0), ("route", 0)] + [("tok", j) for j in range(1, 4)]
            JOBS += [("pick", 0, 0), ("pick", 0, 1), ("weigh", 0)]
            JOBS += [("fetch_up", w, j) for w in range(2) for j in range(16)]
            JOBS += [("first_up", 0)]
            for j in range(16):
                JOBS += [("first_up", j + 1)] * (j < 15) + [("second_up", j)]
            JOBS += [("logits", 1), ("route", 1), ("pick", 1, 0), ("pick", 1, 1), ("weigh", 1)]
            for h in range(2):
                JOBS += [("fetch_down", h, w, j) for j in range(8) for w in range(2 - h)]
                for j in range(8):
                    JOBS += [("first_down", h, j)]
                    if j == 4:
                        JOBS += [("second_down", h, 0)]
                    if h == 0:
                        JOBS += [("fetch_down", 1, 1, j)]
                JOBS += [("second_down", h, 1)]
            JOBS += [("back", w) for w in range(4)]
            number = {job: n for n, job in enumerate(JOBS)}

            def on_act_(job):
                kind = job[0]
                if kind in ("xt", "tok"):
                    return True
                if kind == "fetch_up":
                    return job[1] == 1
                if kind == "fetch_down":
                    return job[2] == 0 and (job[1] == 0 or job[3] % 2 == 0)
                return kind in ("first_up", "first_down") and job[-1] % 2 == 1
            on_act = [on_act_(job) for job in JOBS]

            def emptied(eng, job):
                n = number[job]
                if on_act[n]:
                    eng.wait_ge(by_act, sum(on_act[:n + 1]))
                else:
                    eng.wait_ge(by_dve, n + 1 - sum(on_act[:n + 1]))

            def all_emptied(eng, jobs):
                for who in (False, True):
                    of = [j for j in jobs if on_act[number[j]] == who]
                    if of:
                        emptied(eng, max(of, key=number.get))

            def bank_free(pe, job):
                n = number[job]
                if n >= 8:
                    emptied(pe, JOBS[n - 8])
                return bank[n % 8]

            def fetch(b, rows, cols, table, at, width, picked):
                nc.tensor.matmul(b[rows, cols], self.tab_hm[table][:, at:at + width], picked, start=True, stop=False)
                return nc.tensor.matmul(b[rows, cols], self.tab_lo[table][:, at:at + width], picked,
                                        start=False, stop=True)

            keep_clock = lambda b, n: self.keep_clock(b, n, self.tab_hm["A_up"][:, 0:BANK])

            def up_tokens(j):
                return [(half, 2 * j + e) for half in range(2) for e in range(2)]

            def second_down_part(b, h, j):
                for x in range(4):
                    m2 = 4 * j + x
                    for half in range(2):
                        w = 2 * half + m2 % 2
                        out = b[32 * w:32 * w + 32, :].rearrange("p (d n o) -> p d n o", d=2, n=8)[:, :, (m2 // 2) % 8, :]
                        for k in range(2):
                            pair = h * P + (half * 32 + m2) * 2 + k
                            ins = nc.tensor.matmul(out, fb[:, pair * D1:(pair + 1) * D1],
                                                   diag[:, j % 2, (x * 4 + half * 2 + k) * 64:(x * 4 + half * 2 + k + 1) * 64],
                                                   start=k == 0, stop=k == 1)
                return ins

            @block.tensor
            def _(pe):
                for n, job in enumerate(JOBS):
                    kind = job[0]
                    b = bank_free(pe, job)
                    if kind == "xt":
                        if job[1] == 0:
                            keep_clock(b, BUSY["start"])
                        for t in range(4 * job[1], 4 * job[1] + 4):
                            pe.wait_ge(s["normed"], t + 1)
                            ins = nc.tensor.transpose(b[:, (t % 4) * P:(t % 4 + 1) * P], xn[:, t, :], self.ident[:])
                    elif kind == "tok":
                        for c4 in range(4):
                            for g in range(4):
                                ins = nc.tensor.matmul(b[32 * g:32 * g + 32, c4 * P:(c4 + 1) * P],
                                                       xn[:, 4 * job[1] + g, 32 * c4:32 * c4 + 32], self.ident[:],
                                                       start=True, stop=True)
                    elif job == ("logits", 0):
                        all_emptied(pe, [("xt", j) for j in range(4)])
                        for r in range(TOKROWS):
                            for half in range(2):
                                v = xt[:, 8 * half:8 * half + 8, :].rearrange("c t (n r) -> c (t n) r", r=TOKROWS)
                                ins = nc.tensor.matmul(b[64 * half:64 * half + 64, 0:P], self.router_up[:, r, :],
                                                       v[:, :, r], start=r == 0, stop=r == TOKROWS - 1)
                    elif kind == "logits":
                        spare = bank_free(pe, ("route", 1))
                        keep_clock(spare, BUSY["gelu"])
                        pe.wait_ge(gelu_done, 16)
                        for p in range(F1):
                            if p % 8 == 7:
                                keep_clock(spare, BUSY["logits"])
                            for half in range(2):
                                rows = slice(64 * half, 64 * half + 64)
                                ins = nc.tensor.matmul(b[rows, 0:P], self.router_dn[rows, p, :], hid[rows, :, p],
                                                       start=p == 0, stop=p == F1 - 1)
                    elif kind == "route":
                        emptied(pe, ("logits", job[1]))
                        ins = nc.tensor.transpose(b[:, 0:P], logit_t[:], self.ident[:])
                    elif kind == "pick":
                        _, layer, half = job
                        if layer == 1 and half == 0:
                            keep_clock(b, BUSY["pick"])
                        pe.wait_ge(top_link, ROUTED * (layer + 1))
                        for k in range(2):
                            nc.tensor.transpose(b[:].bitcast(BF16)[:, k * P:(k + 1) * P], one_b[:, half, k, :],
                                                self.identb[:])
                        for k in range(2):
                            ins = nc.tensor.transpose(b[0:EXPERTS, (k + 1) * P:(k + 2) * P], one_w[:, half, k, :],
                                                      self.ident[:])
                    elif kind == "weigh":
                        all_emptied(pe, [("pick", job[1], half) for half in range(2)])
                        for half in range(2):
                            ins = nc.tensor.matmul(b[64 * half:64 * half + 64, :], self.ones[:], pick_w[:],
                                                   start=True, stop=True)
                    elif kind == "fetch_up":
                        _, w, j = job
                        if w == 0:
                            ins = fetch(b, slice(0, P), slice(0, BANK), "A_up", 4 * j * D1, 4 * D1, pick[:, 0, :])
                        else:
                            for o in range(4):
                                for g in range(4):
                                    ins = fetch(b, slice(32 * g, 32 * g + 32), slice(o * P, (o + 1) * P), "B_up",
                                                (4 * j + o) * D1, D1, pick[:, 0, g * P:(g + 1) * P])
                    elif kind == "first_up":
                        j = job[1]
                        if j == 0:
                            keep_clock(b, BUSY["first_up"])
                            all_emptied(pe, [("tok", q) for q in range(4)])
                            all_emptied(pe, [("fetch_up", w, k) for w in range(2) for k in range(16)])
                        for t, (half, e) in enumerate(up_tokens(j)):
                            n_tok = 32 * half + e
                            for g in range(4):
                                rows = slice(32 * g, 32 * g + 32)
                                ins = nc.tensor.matmul(b[rows, t * P:(t + 1) * P], tok[rows, n_tok, :],
                                                       fb[rows, n_tok * P:(n_tok + 1) * P], start=True, stop=True)
                    elif kind == "second_up":
                        j = job[1]
                        emptied(pe, ("first_up", j))
                        if j == 0:
                            keep_clock(b, BUSY["moved"])
                            pe.wait_ge(moved, 16 * 16 * MOVES)
                        for e in range(2):
                            for k in range(2):
                                for half in range(2):
                                    n_tok, t = 32 * half + 2 * j + e, 2 * half + e
                                    ins = nc.tensor.matmul(b[64 * half:64 * half + 64, e * 256:(e + 1) * 256],
                                                           fa_up[:, :, 2 * n_tok + k],
                                                           diag[:, j % 2, (2 * t + k) * 256:(2 * t + k + 1) * 256],
                                                           start=k == 0, stop=k == 1)
                    elif kind == "fetch_down":
                        _, h, w, j = job
                        picked = pick[:, 1, 2 * h * P:(2 * h + 2) * P] if w else \
                            pick[:, 0, :].rearrange("e (c h x) -> e c h x", c=2, h=2)[:, :, h]
                        for jj in range(2):
                            ins = fetch(b, slice(0, P), slice(jj * 256, (jj + 1) * 256),
                                        "B_down" if w else "A_down", (4 * j + 2 * jj) * F1, 2 * F1, picked)
                    elif kind == "first_down":
                        _, h, j = job
                        if j == 0:
                            keep_clock(b, BUSY["first_down"])
                            all_emptied(pe, [("fetch_down", h, w, k) for w in range(2) for k in range(8)])
                        for x in range(4):
                            for d in range(2):
                                m = 8 * j + 2 * x + d
                                ins = nc.tensor.matmul(b[64 * d:64 * d + 64, x * P:(x + 1) * P], hid[:, 64 * h + m, :],
                                                       fa[:, m * P:(m + 1) * P], start=True, stop=True)
                        ins.then_inc(filled, 1)
                        if j:
                            into = ("second_down", h, (j - 1) // 4)
                            if (j - 1) % 4 == 0:
                                bank_free(pe, into)
                            emptied(pe, ("first_down", h, j - 1))
                            ins = second_down_part(bank[number[into] % 8], h, j - 1)
                            if (j - 1) % 4 == 3:
                                ins.then_inc(filled, 1)
                        continue
                    elif kind == "second_down":
                        _, h, part = job
                        if part == 0:
                            continue
                        emptied(pe, ("first_down", h, 7))
                        ins = second_down_part(b, h, 7)
                    elif kind == "back":
                        w = job[1]
                        rows = slice(32 * w, 32 * w + 32)
                        if w == 0:
                            emptied(pe, ("second_down", 1, 1))
                        for q2 in range(2):
                            for d in range(2):
                                v = yt[:, d, q2 * NT:(q2 + 1) * NT, :].rearrange("p n (r c) -> p (n r) c", c=4)
                                for c4 in range(4):
                                    at = (2 * q2 + d) * P + c4 * D1
                                    ins = nc.tensor.transpose(b[:, at:at + D1], v[rows, :, c4], self.ident[rows, rows])
                    ins.then_inc(filled, 1)

            def route(dve, b, layer, done):
                count = [ROUTED * layer]

                def step(*many):
                    for ins in many:
                        count[0] += 1
                        ins.then_inc(top_link, 1)
                    dve.wait_ge(top_link, count[0])

                nc.vector.tensor_copy(logit[:].rearrange("p h e -> p (h e)"), b[:, 0:2 * EXPERTS]).then_inc(by_dve, 1)
                dve.wait_ge(by_dve, done)
                step(*[nc.vector.max(top[:, h, :], logit[:, h, :]) for h in range(2)])
                step(*[nc.vector.max_index(index[:, h, :], top[:, h, :], logit[:, h, :]) for h in range(2)])
                step(nc.vector.tensor_copy(indexf[:], index[:, :, 0:2]),
                     nc.vector.tensor_tensor(gap[:, 0, :], top[:, :, 1], top[:, :, 0], ALU.subtract))
                dve.wait_ge(exp_ready, layer + 1)
                step(nc.vector.tensor_scalar(gap[:, 2, :], gap[:, 1, :], 1.0, None, ALU.add))
                step(nc.vector.reciprocal(gap[:, 2, :], gap[:, 2, :]))
                step(nc.vector.tensor_tensor(gap[:, 3, :], gap[:, 1, :], gap[:, 2, :], ALU.mult))
                for h in range(2):
                    for k in range(2):
                        nc.vector.tensor_scalar(one_w[:, h, k, :], self.iota_e[:, 0:EXPERTS], indexf[:, h, k:k + 1],
                                                gap[:, 2 + k, h:h + 1], ALU.is_equal, ALU.mult).then_inc(top_link, 1)
                        nc.vector.tensor_scalar(one_b[:, h, k, :], self.iota_e[:], indexf[:, h, k:k + 1],
                                                None, ALU.is_equal).then_inc(top_link, 1)
                        count[0] += 2
                assert count[0] == ROUTED * (layer + 1)

            def pick_up(view, half, k):
                return view.rearrange("e (g q t k) -> e q g t k", g=4, q=4, k=2)[:, 2 * half:2 * half + 2, :, :, k]

            def pick_plain(view, half, k):
                return view.rearrange("e (c m k) -> e c m k", c=2, k=2)[:, half, :, k]

            def pick_by_parity(view, half, k):
                return view.rearrange("e (h d c m k) -> e c h m d k", h=2, d=2, c=2, k=2)[:, half, :, :, :, k]

            def move(copy, job, b):
                kind = job[0]
                if kind == "xt":
                    return copy(xt[:, 4 * job[1]:4 * job[1] + 4, :].rearrange("p t r -> p (t r)"), b[:])
                if kind == "tok":
                    return copy(tok[:, NT * job[1]:NT * job[1] + NT, :].rearrange("p t (r c) -> p c (t r)", c=4),
                                b[:].rearrange("p (c r) -> p c r", c=4))
                if kind == "fetch_up":
                    return copy(fb[:].rearrange("p (n o) -> p o n", o=F1)[:, 4 * job[2]:4 * job[2] + 4, :],
                                b[:].rearrange("p (o n) -> p o n", o=4))
                if kind == "fetch_down":
                    for half, odd in ((0, 0), (0, 1), (1, 0), (1, 1)):
                        dst = fa[64 * half:64 * half + 64, :].rearrange("p (m c k o) -> p c o m k", c=2, k=2, o=D1) \
                            [:, half, 4 * job[3] + odd:4 * job[3] + 4:2]
                        src = b[64 * odd:64 * odd + 64, :].rearrange("p (o c m k) -> p o c m k", o=2, c=2, k=2)[:, :, half]
                        ins = copy(dst, src)
                    return ins
                if kind == "first_up":
                    for g in range(4):
                        rows = slice(32 * g, 32 * g + 32)
                        dst = diag[rows, job[1] % 2, :].rearrange("p (t g q) -> p g t q", g=4, q=F1)[:, g]
                        ins = copy(dst, b[rows, :].rearrange("p (t q) -> p t q", q=F1))
                    return ins
                for d in range(2):
                    rows = slice(64 * d, 64 * d + 64)
                    dst = diag[rows, job[2] % 2, 0:1024].rearrange("p (t d q) -> p d t q", d=2, q=D1)[:, d]
                    ins = copy(dst, b[rows, :].rearrange("p (t q) -> p t q", q=D1))
                return ins

            def ready_to_move(eng, job):
                if job[0] == "first_up" and job[1] < 2:
                    eng.wait_ge(zeroed, 1)
                if job[0] == "fetch_down" and job[2] == 0 and job[3] == 0 and job[1] == 0:
                    eng.wait_ge(zeroed, 4)
                if job[0] == "first_down" and job[2] < 2 and job[1] == 0:
                    eng.wait_ge(zeroed, 4)

            @block.vector
            def _(dve):
                self.layernorm_dve(dve, self.x, xn, s)
                done = 0
                for n, job in enumerate(JOBS):
                    if on_act[n]:
                        continue
                    done += 1
                    b = bank[n % 8]
                    kind = job[0]
                    dve.wait_ge(filled, n + 1)
                    ready_to_move(dve, job)
                    if kind == "route":
                        route(dve, b, job[1], done)
                        continue
                    if kind == "logits":
                        ins = nc.vector.tensor_copy(logit_t[:], b[:, 0:P])
                    elif kind == "pick":
                        _, layer, half = job
                        plain, weighted = b[:].bitcast(BF16), b[0:EXPERTS, P:3 * P]
                        for k in range(2):
                            src, src_w = plain[:, k * P:(k + 1) * P], weighted[:, k * P:(k + 1) * P]
                            if layer == 0:
                                cut = lambda v: v.rearrange("e (q g t) -> e q g t", q=2, g=4)
                                nc.vector.tensor_copy(pick_up(pick[:, 0, :], half, k), cut(src))
                                ins = nc.vector.tensor_copy(pick_up(pick_w[:], half, k), cut(src_w))
                            else:
                                cut = lambda v: v.rearrange("e (h m d) -> e h m d", h=2, d=2)
                                nc.vector.tensor_copy(pick_plain(pick[:, 0, :], half, k), src)
                                nc.vector.tensor_copy(pick_by_parity(pick[:, 1, :], half, k), cut(src))
                                ins = nc.vector.tensor_copy(pick_by_parity(pick_w[:], half, k), cut(src_w))
                    elif kind == "weigh":
                        ins = nc.vector.tensor_copy(weight[:], b[:])
                    elif kind == "fetch_up":
                        j = job[2]
                        if j == 0:
                            emptied(dve, ("weigh", 0))
                        ins = nc.vector.tensor_tensor(staged[:, j, :], b[:], weight[:], ALU.mult)
                    elif kind == "fetch_down" and job[2] == 1:
                        _, h, _, j = job
                        if j == 0:
                            emptied(dve, ("weigh", 1))
                        for d, odd in ((0, 0), (0, 1), (1, 0), (1, 1)):
                            dst = fb[64 * d:64 * d + 64, 4096 * h:4096 * h + 4096].rearrange("p (n o) -> p o n", o=D1)[:, 4 * j + odd:4 * j + 4:2]
                            src = b[64 * odd:64 * odd + 64, :].rearrange("p (o d n) -> p o d n", o=2, d=2)[:, :, d]
                            w_pairs = weight[64 * odd:64 * odd + 64, (2 * h + d) * P:(2 * h + d + 1) * P]
                            ins = nc.vector.tensor_tensor(dst, src, w_pairs.unsqueeze(1).broadcast_to([64, 2, P]), ALU.mult)
                    elif kind == "second_up":
                        bias = self.bias_up[:].unsqueeze(1).broadcast_to([P, 8, F1])
                        ins = nc.vector.scalar_tensor_tensor(out=hid[:, 8 * job[1]:8 * job[1] + 8, :],
                                                             in0=b[:].rearrange("p (t o) -> p t o", t=8),
                                                             scalar=self.scale_up[:], in1=bias, op0=ALU.mult, op1=ALU.add)
                    elif kind == "second_down":
                        at = 16 * job[1] + 8 * job[2]
                        for d in range(2):
                            bias = self.bias_dn[:].unsqueeze(1).broadcast_to([P, 8, D1])
                            ins = nc.vector.scalar_tensor_tensor(out=yt[:, d, at:at + 8, :],
                                                                 in0=b[:, d * 256:(d + 1) * 256].rearrange("p (n o) -> p n o", n=8),
                                                                 scalar=self.scale_dn[:], in1=bias, op0=ALU.mult,
                                                                 op1=ALU.add)
                    elif kind == "back":
                        half, gh = job[1] // 2, job[1] % 2
                        xv = self.x[:].rearrange("p (c q g d) e -> p c g q d e", c=2, q=2, g=2)[:, half, gh]
                        ins = nc.vector.tensor_tensor(xv, b[:].rearrange("p (q d e) -> p q d e", q=2, d=2), xv, ALU.add)
                    else:
                        ins = move(nc.vector.tensor_copy, job, b)
                    ins.then_inc(by_dve, 1)

            @block.scalar
            def _(act):
                copy = lambda dst, src: nc.scalar.activation(dst, src, ACT.Copy)
                for n, job in enumerate(JOBS):
                    b = bank[n % 8]
                    if on_act[n]:
                        act.wait_ge(filled, n + 1)
                        ready_to_move(act, job)
                        move(copy, job, b).then_inc(by_act, 1)
                    elif job[0] == "route":
                        act.wait_ge(top_link, ROUTED * job[1] + 6)
                        nc.scalar.activation(gap[:, 1, :], gap[:, 0, :], ACT.Exp).then_inc(exp_ready, 1)
                    elif job[0] == "second_up":
                        emptied(act, job)
                        v = hid[:, 8 * job[1]:8 * job[1] + 8, :]
                        nc.scalar.activation(v, v, ACT.Gelu).then_inc(gelu_done, 1)

            @block.gpsimd
            def _(pool):
                nc.gpsimd.memset(diag[:], 0.0).then_inc(zeroed, 1)
                self.layernorm_pool(pool, s)
                pool.wait_ge(filled, number[("second_up", 15)] + 1)
                nc.gpsimd.memset(diag[:, :, 0:1024], 0.0).then_inc(zeroed, 1)
                for half in range(2):
                    pool.wait_ge(zeroed, 2 + half)
                    rows = slice(64 * half, 64 * half + 64)
                    v = fa[rows, :].rearrange("p (m c q) -> p c m q", c=2, q=2 * D1)[:, 1 - half]
                    nc.gpsimd.memset(v, 0.0).then_inc(zeroed, 1)

            @block.sync
            def _(sp):
                for m in range(MOVES):
                    at = slice(16 // MOVES * m, 16 // MOVES * (m + 1))
                    emptied(sp, ("fetch_up", 0, at.stop - 1))
                    for o in range(4):
                        for g in range(4):
                            dst = fa_up[32 * g:32 * g + 32].rearrange("p (j o) n -> p j o n", o=4)[:, at, o]
                            sp.dma_start(dst, staged[32 * o:32 * o + 32, at, g * P:(g + 1) * P]).then_inc(moved, 16)
                sp.wait_ge(moved, 16 * 16 * MOVES)
                if final:
                    out_rows = self.out.rearrange("b (t p) d -> p (b t) d", p=P)
                    for w in range(4):
                        emptied(sp, ("back", w))
                        for q2 in range(2):
                            at = 8 * (w // 2) + 4 * q2 + 2 * (w % 2)
                            sp.dma_start(out_rows[:, at:at + 2, :], self.x[:, at:at + 2, :]).then_inc(stored, 16)
                    sp.wait_ge(stored, 8 * 16)

    def build(self):
        nc = self.nc
        self.scratch_qkv = nc.dram_tensor("scratch_qkv", [BATCH * SEQ, 3 * D], F32, kind="Internal").ap()
        self.scratch_y = nc.dram_tensor("scratch_y", [BATCH * SEQ * D], F32, kind="Internal").ap()
        with ExitStack() as ctx:
            self.setup(ctx)
            for causal in (False, True):
                with ExitStack() as c:
                    y = self.sb(c, "y", [P, QUADS, 4, TPB, HD])
                    qkv = self.sb(c, "qkv", [P, QUADS, 4 * TPB, 24])
                    self.attention_inputs(c)
                    if not causal:
                        self.table_buffers(c)
                    self.project(causal, qkv)
                    self.attention(causal, qkv, y)
                self.mixture(final=causal)


_INS = ["L0_attn_a_x", "L0_attn_a_ln_g", "L0_attn_a_ln_b", "L0_attn_a_Wq", "L0_attn_a_bq", "L0_attn_a_Wk",
        "L0_attn_a_bk", "L0_attn_a_Wv", "L0_attn_a_bv", "L0_attn_b_qkv_kernel", "L0_attn_b_qkv_bias",
        "L0_ffn_W_up", "L0_ffn_A_up", "L0_ffn_B_up", "L0_ffn_scale_up", "L0_ffn_bias_up", "L0_ffn_W_down",
        "L0_ffn_A_down", "L0_ffn_B_down", "L0_ffn_scale_down", "L0_ffn_bias_down"]


def kernel(**inputs):
    import numpy as _np
    import concourse.bacc as _bacc
    from concourse import mybir as _mybir
    from concourse.bass_utils import run_bass_kernel_spmd as _run

    nc = _bacc.Bacc("TRN2", target_bir_lowering=False, num_devices=1)
    arrays, aps = {}, {}
    for name in _INS:
        a = _np.ascontiguousarray(inputs[name])
        arrays[f"in_{name}"] = a
        aps[name] = nc.dram_tensor(f"in_{name}", a.shape, _mybir.dt.from_np(a.dtype), kind="ExternalInput").ap()
    out = nc.dram_tensor("out_0", (BATCH, SEQ, D), F32, kind="ExternalOutput").ap()
    Kernel(nc, aps, out).build()
    r = _run(nc, [arrays], core_ids=[0])
    return r.results[0]["out_0"]
```
